# Optimizing a Trainium2 kernel written in Bass

```python
import numpy as np
import jax
import jax.numpy as jnp

def _softmax(x, axis=-1):
    return jax.nn.softmax(x, axis=axis)

def _gelu(x):
    return jax.nn.gelu(x, approximate=True)

def _silu(x):
    return jax.nn.silu(x)

def _sigmoid(x):
    return jax.nn.sigmoid(x)

def _layernorm(x, axis=-1, eps=1e-05):
    m = jnp.mean(x, axis=axis, keepdims=True)
    v = jnp.var(x, axis=axis, keepdims=True)
    return (x - m) / jnp.sqrt(v + eps)

def _scatter_add(tgt, idx, src, axis=0):
    return tgt.at[idx].add(src)

def _segment_sum(src, seg, n):
    return jax.ops.segment_sum(src, seg, n)
kernel_name = 'mk_xattn_ffn_d1_seqx_r4_b8bc81'

def setup_inputs(seed: int=0):
    np.random.seed(seed)
    _w = jnp.asarray

    def _rec_inputs():
        import jax
        import jax.numpy as jnp
        _rk = jax.random.key(seed)
        x = -0.0005207 + 1.001 * jax.random.normal(jax.random.fold_in(_rk, 1), (8, 112, 1024), jnp.float32)
        _lenS = 112 - jax.random.randint(jax.random.fold_in(_rk, 7), (8,), 0, max(1, 112 // 4) + 1, jnp.int32)
        _lenS2 = 375 - jax.random.randint(jax.random.fold_in(_rk, 8), (8,), 0, max(1, 375 // 4) + 1, jnp.int32)
        _ctx_4096P = jax.random.normal(jax.random.fold_in(_rk, 11), (8, 16, 1024), jnp.float32)
        _ctx_4096c = jax.random.dirichlet(jax.random.fold_in(_rk, 511), 0.3 * jnp.ones((16,), jnp.float32), (8, 375))
        _ctx_4096t = jnp.einsum('bsk,bkd->bsd', _ctx_4096c, _ctx_4096P)
        _ctx_4096t = _ctx_4096t * jax.lax.rsqrt(jnp.mean(jnp.square(_ctx_4096t)) + 1e-12) * 0.953939
        ctx_4096 = -0.00010331 + 0.999899 * (_ctx_4096t + 0.3 * jax.random.normal(jax.random.fold_in(_rk, 611), (8, 375, 1024), jnp.float32))
        return (x, ctx_4096)
    x, ctx_4096 = _rec_inputs()

    def _L0_xattn_setup():
        import jax, jax.numpy as jnp
        import numpy as np
        import math
        HIDDEN = 1024
        N_HEADS = 32
        HEAD_DIM = 128
        N_KV_HEADS = 4
        N_GROUPS = N_HEADS // N_KV_HEADS
        key = jax.random.key(seed)
        ks = jax.random.split(key, 6)
        B, NL, S = (8, 64, 1024)
        latents = jax.random.normal(ks[0], (B, NL, HIDDEN), dtype=jnp.float32)
        context = jax.random.normal(ks[1], (B, S, HIDDEN), dtype=jnp.float32)
        scale = 1.0 / math.sqrt(HIDDEN)
        Wq = jax.random.normal(ks[2], (HIDDEN, N_HEADS * HEAD_DIM), dtype=jnp.float32) * scale
        Wk = jax.random.normal(ks[3], (HIDDEN, N_KV_HEADS * HEAD_DIM), dtype=jnp.float32) * scale
        Wv = jax.random.normal(ks[4], (HIDDEN, N_KV_HEADS * HEAD_DIM), dtype=jnp.float32) * scale
        Wo = jax.random.normal(ks[5], (N_HEADS * HEAD_DIM, HIDDEN), dtype=jnp.float32) * scale
        return {'latents': latents, 'context': context, 'Wq': Wq, 'Wk': Wk, 'Wv': Wv, 'Wo': Wo}
    _L0_xattn_all = _L0_xattn_setup()
    _L0_xattn_in = {k: v for k, v in _L0_xattn_all.items() if k in ('Wq', 'Wk', 'Wv', 'Wo')}
    del _L0_xattn_all

    def _L0_ffn_setup():
        import jax, jax.numpy as jnp
        import numpy as np
        HID, INT, LAT, NE, K = (1024, 2048, 512, 8, 2)
        LN_EPS = 1e-05

        def _layernorm(x, gamma, beta):
            mu = jnp.mean(x, axis=-1, keepdims=True)
            var = jnp.var(x, axis=-1, keepdims=True)
            return (x - mu) * jax.lax.rsqrt(var + LN_EPS) * gamma + beta
        key = jax.random.key(seed)
        ks = jax.random.split(key, 8)
        s = lambda d: 1.0 / np.sqrt(d)
        return {'hidden_states': jax.random.normal(ks[0], (4, 512, HID), jnp.float32), 'gate_w': jax.random.normal(ks[1], (HID, NE), jnp.float32) * s(HID), 'up_w': jax.random.normal(ks[2], (HID, INT), jnp.float32) * s(HID), 'down_w': jax.random.normal(ks[3], (INT, HID), jnp.float32) * s(INT), 'fc1_w': jax.random.normal(ks[4], (HID, LAT), jnp.float32) * s(HID), 'fc2_w': jax.random.normal(ks[5], (LAT, HID), jnp.float32) * s(LAT), 'expert_w': jax.random.normal(ks[6], (LAT, LAT), jnp.float32), 'ln_gamma': jnp.ones((HID,), jnp.float32), 'ln_beta': jnp.zeros((HID,), jnp.float32)}
    _L0_ffn_all = _L0_ffn_setup()
    _L0_ffn_in = {k: v for k, v in _L0_ffn_all.items() if k in ('gate_w', 'up_w', 'down_w', 'fc1_w', 'fc2_w', 'expert_w', 'ln_gamma', 'ln_beta')}
    del _L0_ffn_all
    return {'x': x, 'ctx_4096': ctx_4096, 'L0_xattn_Wq': _L0_xattn_in['Wq'], 'L0_xattn_Wk': _L0_xattn_in['Wk'], 'L0_xattn_Wv': _L0_xattn_in['Wv'], 'L0_xattn_Wo': _L0_xattn_in['Wo'], 'L0_ffn_gate_w': _L0_ffn_in['gate_w'], 'L0_ffn_up_w': _L0_ffn_in['up_w'], 'L0_ffn_down_w': _L0_ffn_in['down_w'], 'L0_ffn_fc1_w': _L0_ffn_in['fc1_w'], 'L0_ffn_fc2_w': _L0_ffn_in['fc2_w'], 'L0_ffn_expert_w': _L0_ffn_in['expert_w'], 'L0_ffn_ln_gamma': _L0_ffn_in['ln_gamma'], 'L0_ffn_ln_beta': _L0_ffn_in['ln_beta']}

def reference(x, ctx_4096, L0_xattn_Wq, L0_xattn_Wk, L0_xattn_Wv, L0_xattn_Wo, L0_ffn_gate_w, L0_ffn_up_w, L0_ffn_down_w, L0_ffn_fc1_w, L0_ffn_fc2_w, L0_ffn_expert_w, L0_ffn_ln_gamma, L0_ffn_ln_beta):
    import jax
    import jax.numpy as jnp

    def _L0_xattn_ref(latents, context, Wq, Wk, Wv, Wo):
        import jax, jax.numpy as jnp
        import numpy as np
        import math
        HIDDEN = 1024
        N_HEADS = 32
        HEAD_DIM = 128
        N_KV_HEADS = 4
        N_GROUPS = N_HEADS // N_KV_HEADS
        b, q_len, _ = latents.shape
        kv_len = q_len + context.shape[1]
        hidden_states = jnp.concatenate([context, latents], axis=1)
        q = (latents @ Wq).reshape(b, q_len, N_KV_HEADS, N_GROUPS, HEAD_DIM)
        k = (hidden_states @ Wk).reshape(b, kv_len, N_KV_HEADS, HEAD_DIM)
        v = (hidden_states @ Wv).reshape(b, kv_len, N_KV_HEADS, HEAD_DIM)
        scale = 1.0 / math.sqrt(HEAD_DIM)
        scores = jnp.einsum('bqhgd,bkhd->bhgqk', q, k) * scale
        attn = jax.nn.softmax(scores.astype(jnp.float32), axis=-1).astype(q.dtype)
        out = jnp.einsum('bhgqk,bkhd->bqhgd', attn, v)
        out = out.reshape(b, q_len, N_HEADS * HEAD_DIM)
        return out @ Wo

    def _L0_ffn_ref(hidden_states, gate_w, up_w, down_w, fc1_w, fc2_w, expert_w, ln_gamma, ln_beta):
        import jax, jax.numpy as jnp
        import numpy as np
        HID, INT, LAT, NE, K = (1024, 2048, 512, 8, 2)
        LN_EPS = 1e-05

        def _layernorm(x, gamma, beta):
            mu = jnp.mean(x, axis=-1, keepdims=True)
            var = jnp.var(x, axis=-1, keepdims=True)
            return (x - mu) * jax.lax.rsqrt(var + LN_EPS) * gamma + beta
        logits = jnp.einsum('bsh,he->bse', hidden_states, gate_w)
        routing_weights, selected_experts = jax.lax.top_k(logits, K)
        h = jax.nn.relu(jnp.einsum('bsh,hi->bsi', hidden_states, up_w)) ** 2
        shared_out = jnp.einsum('bsi,ih->bsh', h, down_w)
        x_latent = jnp.einsum('bsh,hl->bsl', hidden_states, fc1_w)
        expert_out = jnp.einsum('bsl,lm->bsm', x_latent, expert_w)
        moe_out = expert_out * jnp.sum(routing_weights, axis=-1, keepdims=True)
        routed_out = jnp.einsum('bsl,lh->bsh', moe_out, fc2_w)
        return _layernorm(shared_out + routed_out, ln_gamma, ln_beta)
    x = x + _L0_xattn_ref(_layernorm(x, axis=-1), ctx_4096, L0_xattn_Wq, L0_xattn_Wk, L0_xattn_Wv, L0_xattn_Wo)
    x = x + _L0_ffn_ref(_layernorm(x, axis=-1), L0_ffn_gate_w, L0_ffn_up_w, L0_ffn_down_w, L0_ffn_fc1_w, L0_ffn_fc2_w, L0_ffn_expert_w, L0_ffn_ln_gamma, L0_ffn_ln_beta)
    return x

_drawn_inputs = setup_inputs


def setup_inputs(seed=0):
    import zlib

    import numpy as np

    out = dict(_drawn_inputs(seed))
    spreads = {'L0_ffn_ln_gamma': (1.0, 0.2), 'L0_ffn_ln_beta': (0.0, 0.1)}
    factors = {}
    for name, (base, spread) in spreads.items():
        noise = np.random.default_rng([zlib.crc32(name.encode()), seed]).standard_normal(out[name].shape)
        drawn = base * np.exp(spread * noise) if base else spread * noise
        out[name] = jnp.asarray(drawn.astype(out[name].dtype))
    for name, factor in factors.items():
        out[name] = (out[name] * factor).astype(out[name].dtype)
    return out
```

```python
from contextlib import ExitStack

import concourse.bass as bass
from concourse import mybir

F32 = mybir.dt.float32
F32R = mybir.dt.float32r
ALU = mybir.AluOpType
ACT = mybir.ActivationFunctionType
AX = mybir.AxisListType

P = 128
B, SQ, HID = 8, 112, 1024
SC = 375
NH, NKV, D = 32, 4, 128
G = NH // NKV
INT, LAT, NE = 2048, 512, 8
KEYS = SC + SQ
KP = 488
KT = KP // 4
ROWS = B * SQ
RT = ROWS // P
HALF = ROWS // 2
NK = HID // P
QC = G * SQ
QT = QC // P
QA = 4 * P
SLAB = NK * P
SCALE = float(D) ** -0.5
FREE = 16
EPS = 1e-5

T_Q = 0
T_WO = T_Q + NH
T_FC1 = T_WO + NKV * NK
T_EXP = T_FC1 + LAT // P
T_FC2 = T_EXP + LAT // P // 2
T_FFN = T_FC2 + HID // P // 2
N_SLABS = T_FFN + 4 * NK

C_LN1 = 0
C_Q = C_LN1 + 2 * RT
C_KV = C_Q + 2 * NH
C_WO = C_KV + 8 * B
C_LN2 = C_WO + NKV * 2 * NK
C_FC1 = C_LN2 + 4 * RT
C_GATE = C_FC1 + 2 * (LAT // P)
C_EXP = C_GATE + 5
C_FC2 = C_EXP + 2 * (LAT // P)
C_FFN = C_FC2 + 2 * NK
C_LN3 = C_FFN + 8 * NK
C_END = C_LN3 + 2 * RT

H_LN1 = 0
H_Q = H_LN1 + 2 * RT
H_KV = H_Q + 2 * NH
H_LN2 = H_KV + 8 * B
H_FC1 = H_LN2 + 2 * RT
H_EXP = H_FC1 + 2 * (LAT // P)
H_FFN = H_EXP + 2 * (LAT // P)
L_EXP = 0
L_FFN = L_EXP + 2 * (LAT // P)

LN2_GROUPS = [(what, r - (what == "n"), h) for r in range(RT + 1) for what in "yn" for h in range(2)
              if 0 <= r - (what == "n") < RT]


def xattn_ffn(nc, x, ctxT, slabs, wkv, gate, gamma, beta, out):
    with ExitStack() as top:
        def sb(name, cols, dt=F32):
            return top.enter_context(nc.sbuf_tensor(name, [P, cols], dt))

        def sem(name):
            return top.enter_context(nc.semaphore(name))

        def sems(name, n):
            return [sem(f"{name}{j}") for j in range(n)]

        def dram(name, shape):
            return nc.dram_tensor(name, shape, F32).ap()

        xt_d = dram("xt_scratch", (B, P, 2, NK, SQ))
        q_d = dram("q_scratch", (NKV * B, P, 2, G, SQ))
        k_d = dram("k_scratch", (NKV, B, P, 2 * KP))
        v_d = dram("v_scratch", (NKV, B, KT, 2, 4, D))
        k_f = k_d.rearrange("h b p c -> (h b) p c")
        v_f = v_d.rearrange("h b p l t d -> (h b) p (l t d)")
        q_f = q_d.rearrange("n p l g s -> n p (l g s)")
        x2_d = dram("x2_beta_scratch", (ROWS, HID))

        RA = sb("act_region", 2 * 2 * NK * KP, F32R)
        RB = sb("mid_region", 16384, F32R)
        RC = sb("slab_split", 4 * SLAB, F32R)
        RD = sb("small_region", 2048, F32R)
        RAW = sb("slab_raw", 2 * SLAB)
        FB = sb("tile_region", 4096)
        YR = sb("y_region", NK * ROWS)
        ident = sb("ident", P)
        ones = sb("ones", P)
        gate_raw = sb("gate_raw", NK * NE)
        small = sb("small", 224)

        def part(t, at, n):
            return t[:, at:at + n]

        XT = [part(RA, l * NK * ROWS, NK * ROWS).rearrange("p (k n) -> p k n", k=NK) for l in range(2)]
        AT = [part(RA, l * NK * ROWS, NK * ROWS).rearrange("p (b g s) -> p b g s", b=B, g=G) for l in range(2)]
        ATf = [part(RA, l * NK * ROWS, NK * ROWS).rearrange("p (b c) -> p b c", b=B) for l in range(2)]
        HT = [[part(RA, (2 * j + l) * NK * KP, NK * KP).rearrange("p (k n) -> p k n", k=NK)
               for l in range(2)] for j in range(2)]
        PIECE = 2 * 512
        WKV = [[part(RB, (2 * j + l) * PIECE, PIECE) for l in range(2)] for j in range(8)]
        QST = [[part(RB, 12 * PIECE + (2 * s + l) * ROWS, ROWS) for l in range(2)] for s in range(2)]
        PT = [part(RB, l * 4 * QC, 4 * QC).rearrange("p (t n) -> p t n", t=4) for l in range(2)]
        at = 8 * QC
        QB = [part(RB, at + s * 2 * QC, 2 * QC) for s in range(2)]
        at += 4 * QC
        KB = [part(RB, at + s * 2 * KP, 2 * KP) for s in range(2)]
        at += 4 * KP
        VB = [part(RB, at + s * 8 * D, 8 * D) for s in range(2)]
        IN = [part(RB, l * NK * ROWS, NK * ROWS).rearrange("p (k n) -> p k n", k=NK) for l in range(2)]
        WS = [[part(RC, (2 * s + l) * SLAB, SLAB) for l in range(2)] for s in range(2)]
        KVST = [[part(RD, (2 * s + l) * 512, 512) for l in range(2)] for s in range(2)]
        GT = [part(RD, l * NK * P, NK * P).rearrange("p (k n) -> p k n", k=NK) for l in range(2)]
        RAWS = [part(RAW, s * SLAB, SLAB) for s in range(2)]
        PRAW = [part(FB, s * PIECE, PIECE) for s in range(3)] * 2 + [part(YR, s * PIECE, PIECE) for s in range(2)]
        CRAW = part(FB, 0, NK * SC).rearrange("p (k n) -> p k n", k=NK)
        PR = [part(FB, i * KP, KP) for i in range(QT)]
        XIN = [part(FB, s * HID, HID) for s in range(2)]
        XN = part(FB, 2 * HID, HID)
        BETA = part(FB, 3 * HID, HID)
        RWREP = part(FB, 0, QC).rearrange("p (r n) -> p r n", r=RT)
        LGT = part(FB, ROWS, ROWS)
        RWB = part(FB, 2048, ROWS)
        RELU = part(FB, 3008, HALF)
        SQT = part(FB, 3456, HALF)
        GAMMA = part(FB, 0, HID)
        XB = [part(FB, (1 + s) * HID, HID) for s in range(2)]
        CEN = part(FB, 3 * HID, HID)
        X7 = YR[:, :].rearrange("p (r n) -> p r n", r=RT)
        Y = YR[:, :].rearrange("p (k n) -> p k n", k=NK)
        stats = small[:, 0:12]
        mv = small[:, 16:16 + 2 * RT].rearrange("p (r c) -> p r c", c=2)
        sd = small[:, 32:32 + RT]
        rs = small[:, 40:40 + RT]
        negmax = small[:, 48:48 + QT]
        rowsum = small[:, 56:56 + QT]
        rrow = small[:, 64:64 + QT]
        rw = small[:, 72:72 + RT]
        lg = small[:, 80:80 + RT * NE]
        top8 = small[:, 144:144 + RT * NE]

        bank = [top.enter_context(nc.psum_tensor(f"bank{j}", [P, 512], F32)) for j in range(8)]
        GB = [bank[7], bank[3], bank[4], bank[5]]
        SB, TB, AV = bank[0:3], bank[3:5], bank[5:7]

        def gb(c):
            return GB[c % 4]

        s_x = sems("x_loaded", RT)
        s_raw = sems("slab_loaded", 2)
        s_piece = sems("kv_piece_loaded", 5)
        s_ctx = sem("ctx_loaded")
        s_lat = sems("latents_loaded", 2)
        s_xt = sem("xt_stored")
        s_qst = sems("q_stored", 2)
        s_kvst = sems("kv_stored", 2)
        s_qk = sems("qk_loaded", 2)
        s_v = sems("v_loaded", 2)
        s_xin = sems("x_again", 2)
        s_x2st = sems("x2_stored", 2)
        s_misc = sem("gate_beta_loaded")
        s_gamma = sem("gamma_loaded")
        s_out = sems("out_stored", 2)
        s_const = sem("consts_made")
        s_agg = sem("stats_done")
        s_sd = sem("sd_done")
        s_link = sem("vector_chain")
        s_xn = sem("rows_normalised")
        s_mm = sem("group_done")
        s_hi = sem("hi_of_group")
        s_ev = sem("group_taken")
        s_lo = sem("lo_of_tile")
        s_relu = sem("relu_done")
        s_whi = sem("slab_hi")
        s_wlo = sem("slab_lo")
        s_phi = sem("piece_hi")
        s_plo = sem("piece_lo")
        s_chi = sem("ctx_hi")
        s_clo = sem("ctx_lo")
        s_pad = sem("pad_zeroed")
        s_s = sem("scores_done")
        s_max = sem("max_done")
        s_exp = sem("exp_done")
        s_rec = sem("reciprocal_done")
        s_pn = sem("p_normalised")
        s_t = sem("pT_done")
        s_pth = sem("pT_hi")
        s_ptl = sem("pT_lo")
        s_av = sem("av_done")
        s_avh = sem("av_hi")
        s_avl = sem("av_lo")
        s_zero = sem("y_zeroed")
        s_gz = sem("gate_zeroed")
        s_gs = sem("gate_split")
        s_x2 = sem("x2_summed")
        s_x2b = sem("x2_beta")
        s_rw = sem("routing_weight")
        s_o = sem("out_tile")

        top.enter_context(nc.allow_non_contiguous_dma(reason="scratch rows of 448 bytes"))
        block = top.enter_context(nc.Block())

        def f32(ap):
            return ap.bitcast(F32)

        @block.sync
        def _(sp):
            def slab_raw(t, s, n):
                sp.wait_ge(s_wlo, n + 1)
                sp.dma_start(RAWS[s], slabs[t]).then_inc(s_raw[s], 16)

            for r in range(RT):
                sp.dma_start(X7[:, r, :], x[r * P:(r + 1) * P, :]).then_inc(s_x[r], 16)
                if r == 1:
                    for s in range(2):
                        sp.dma_start(RAWS[s], slabs[s]).then_inc(s_raw[s], 16)
            for j in range(6):
                if j >= 3:
                    sp.wait_ge(s_plo, j - 2)
                sp.dma_start(PRAW[j], wkv[j]).then_inc(s_piece[j % 3], 16)
            sp.wait_ge(s_ev, C_Q)
            for l in range(2):
                for b in range(B):
                    sp.dma_start(xt_d[b, :, l], f32(XT[l][:, :, b * SQ:(b + 1) * SQ])).then_inc(s_xt, 16)
            for j in range(6, 8):
                sp.dma_start(PRAW[j], wkv[j]).then_inc(s_piece[j - 3], 16)
            sp.wait_ge(s_plo, 6)
            sp.dma_start(CRAW, ctxT[0]).then_inc(s_ctx, 16)

            with sp.Fori(0, NKV) as kv:
                for g in range(G):
                    m, s = kv * G + g, g % 2
                    slab_raw(T_Q + m + 2, s, T_Q + m)
                    sp.wait_ge(s_ev, C_Q + 2 * m + 2)
                    for l in range(2):
                        sp.dma_start(q_d[bass.ds(kv * B, B), :, l, g, :].rearrange("b p s -> p b s"),
                                     f32(QST[s][l]).rearrange("p (b s) -> p b s", b=B)).then_inc(s_qst[s], 16)

            def latents(b, j):
                for l in range(2):
                    sp.dma_start(f32(HT[j][l][:, :, SC:KEYS]), xt_d[b, :, l]).then_inc(s_lat[j], 16)

            def kv_batch(b, j, more):
                if more:
                    sp.wait_ge(s_mm, C_KV + 8 * b)
                    latents(b + 1, 1 - j)
                    sp.wait_ge(s_clo, b + 1)
                    sp.dma_start(CRAW, ctxT[b + 1]).then_inc(s_ctx, 16)
                for u in range(8):
                    s = u % 2
                    sp.wait_ge(s_ev, C_KV + 8 * b + u + 1)
                    if u < 4:
                        dst, src = k_d[u, b], part(RD, s * 1024, 1024)
                        sp.dma_start(dst.rearrange("p (l c) -> p l c", l=2),
                                     f32(src).rearrange("p (l c) -> p l c", l=2)[:, :, 0:KP]).then_inc(s_kvst[s], 16)
                    else:
                        for l in range(2):
                            sp.dma_start(v_d[:, b, :, l, u - 4, :].rearrange("h p d -> p h d"),
                                         f32(KVST[s][l])[0:KT, :].rearrange("p (h d) -> p h d", h=NKV)
                                         ).then_inc(s_kvst[s], 16)

            sp.wait_ge(s_mm, C_KV)
            sp.wait_ge(s_xt, 16 * 2 * B)
            latents(0, 0)
            with sp.Fori(0, B // 2 - 1) as i:
                for j in range(2):
                    kv_batch(2 * i + j, j, True)
            kv_batch(B - 2, 0, True)
            kv_batch(B - 1, 1, False)

            def load_qk(n, s):
                sp.dma_start(f32(QB[s]), q_f[n]).then_inc(s_qk[s], 16)
                sp.dma_start(f32(KB[s]), k_f[n]).then_inc(s_qk[s], 16)

            def load_v(n, s):
                sp.dma_start(f32(VB[s])[0:KT, :], v_f[n]).then_inc(s_v[s], 16)

            sp.wait_ge(s_mm, C_WO)
            for s in range(2):
                sp.wait_ge(s_qst[s], FREE + 16 * 2 * NH // 2)
                sp.wait_ge(s_kvst[s], FREE + 16 * B * (2 + 4))
            for n in range(2):
                load_qk(n, n)
                load_v(n, n)

            def attention_loads(n, s):
                sp.wait_ge(s_s, QT * n)
                load_qk(n + 1, 1 - s)
                sp.wait_ge(s_av, 2 * n)
                load_v(n + 1, 1 - s)

            def wo_loads(kv):
                with sp.Fori(0, NK // 2) as i:
                    for s in range(2):
                        t = T_WO + kv * NK + 2 * i + s
                        slab_raw(t + 2, s, t)

            with sp.Fori(0, NKV - 1) as kv:
                with sp.Fori(0, B // 2) as i:
                    for j in range(2):
                        attention_loads(kv * B + 2 * i + j + 1, 1 - j)
                wo_loads(kv)
            with sp.Fori(0, B // 2 - 1) as i:
                for j in range(2):
                    attention_loads((NKV - 1) * B + 2 * i + j + 1, 1 - j)
            sp.wait_ge(s_t, QT * NKV * B)
            sp.dma_start(BETA, beta.partition_broadcast(P)).then_inc(s_misc, 16)
            sp.dma_start(gate_raw[:, :], gate).then_inc(s_misc, 16)
            for s in range(2):
                sp.dma_start(XIN[s], x[s * P:(s + 1) * P, :]).then_inc(s_xin[s], 16)
            wo_loads(NKV - 1)

            for r in range(RT):
                sp.wait_ge(s_x2b, r + 1)
                sp.dma_start(x2_d[r * P:(r + 1) * P, :], XIN[r % 2]).then_inc(s_x2st[r % 2], 16)
                if r + 2 < RT:
                    sp.wait_ge(s_x2st[r % 2], 16 * (r // 2 + 1))
                    sp.dma_start(XIN[r % 2], x[(r + 2) * P:(r + 3) * P, :]).then_inc(s_xin[r % 2], 16)

            with sp.Fori(0, (N_SLABS - T_FC1) // 2 - 1) as i:
                for s in range(2):
                    t = T_FC1 + 2 * i + s
                    slab_raw(t + 2, s, t)

            sp.wait_ge(s_lo, L_FFN + 4 * NK)
            for s in range(2):
                sp.wait_ge(s_x2st[s], 16 * ((RT + 1 - s) // 2))
            sp.dma_start(GAMMA, gamma.partition_broadcast(P)).then_inc(s_gamma, 16)
            for r in range(RT):
                s = r % 2
                if r >= 2:
                    sp.wait_ge(s_out[s], 16 * (r // 2))
                sp.dma_start(XB[s], x2_d[r * P:(r + 1) * P, :]).then_inc(s_xin[s], 16)
                if r >= 1:
                    sp.wait_ge(s_o, r)
                    sp.dma_start(out[(r - 1) * P:r * P, :], XB[1 - s]).then_inc(s_out[1 - s], 16)
            sp.wait_ge(s_o, RT)
            sp.dma_start(out[(RT - 1) * P:RT * P, :], XB[(RT - 1) % 2]).then_inc(s_out[(RT - 1) % 2], 16)
            for s in range(2):
                sp.wait_ge(s_out[s], 16 * ((RT + 1 - s) // 2))

        @block.gpsimd
        def _(pool):
            pool.memset(ident[:, :], 0.0).then_inc(s_const, 1)
            pool.memset(ones[:, :], 1.0).then_inc(s_const, 1)
            pool.wait_ge(s_const, 2)
            pool.affine_select(out=ident[:, :], in_=ident[:, :], compare_op=ALU.not_equal, fill=1.0, base=0,
                               pattern=[[-1, P]], channel_multiplier=1).then_inc(s_const, 1)

            for n, (free, count) in enumerate([*((q, FREE) for q in (*s_qst, *s_kvst)), (s_avl, 1)]):
                pool.memset(small[:, 212 + n:213 + n], 0.0).then_inc(free, count)

            def slab_lo(t, s):
                pool.wait_ge(s_whi, t + 1)
                pool.tensor_tensor(WS[s][1], RAWS[s], f32(WS[s][0]), ALU.subtract).then_inc(s_wlo, 1)

            def slabs_lo(t0, n):
                with pool.Fori(0, n // 2) as i:
                    for j in range(2):
                        slab_lo(t0 + 2 * i + j, 1 - j)

            def ctx_lo(b, j):
                pool.wait_ge(s_chi, b + 1)
                pool.tensor_tensor(HT[j][1][:, :, 0:SC], CRAW, f32(HT[j][0][:, :, 0:SC]),
                                   ALU.subtract).then_inc(s_clo, 1)

            slab_lo(0, 0)
            slabs_lo(1, NH)
            pool.wait_ge(s_mm, C_KV)
            pool.wait_ge(s_xt, 16 * 2 * B)
            for j in range(2):
                for l in range(2):
                    pool.memset(f32(HT[j][l][:, :, KEYS:KP]), 0.0).then_inc(s_pad, 1)
            with pool.Fori(0, B // 2) as i:
                for j in range(2):
                    ctx_lo(2 * i + j, j)
            pool.wait_ge(s_plo, 8)
            pool.memset(YR[:, :], 0.0).then_inc(s_zero, 1)
            pool.wait_ge(s_clo, B)
            pool.memset(FB[:, 0:QT * KP].rearrange("p (i c) -> p i c", i=QT)[:, :, KEYS:KP], 0.0).then_inc(s_zero, 1)
            for s in range(2):
                pool.wait_ge(s_kvst[s], FREE + 16 * B * (2 + 4))
            pool.memset(f32(RD[:, :]), 0.0).then_inc(s_gz, 1)

            def p_normalise(n):
                for i in range(QT):
                    pool.wait_ge(s_rec, QT * n + i + 1)
                    pool.tensor_tensor(PR[i], PR[i], rrow[:, i:i + 1].broadcast_to([P, KP]),
                                       ALU.mult).then_inc(s_pn, 1)

            p_normalise(0)
            with pool.Fori(0, NKV - 1) as kv:
                with pool.Fori(0, B) as i:
                    p_normalise(kv * B + i + 1)
                slabs_lo(T_WO + 1 + kv * NK, NK)
            with pool.Fori(0, B - 1) as i:
                p_normalise((NKV - 1) * B + i + 1)
            slabs_lo(T_WO + 1 + (NKV - 1) * NK, NK)
            pool.wait_ge(s_misc, 32)
            for r in range(RT):
                pool.wait_ge(s_xn, RT + r + 1)
                pool.tensor_tensor(XIN[r % 2], XIN[r % 2], BETA, ALU.add).then_inc(s_x2b, 1)
            slabs_lo(T_FC1 + 1, N_SLABS - T_FC1 - 2)
            slab_lo(N_SLABS - 1, 1)

        @block.scalar
        def _(act):
            def slab_hi(t, s, c):
                act.wait_ge(s_raw[s], 16 * (t // 2 + 1) if isinstance(t, int) else t[1])
                act.wait_ge(s_mm, c)
                act.activation(WS[s][0], RAWS[s], ACT.Copy).then_inc(s_whi, 1)

            def loads(t0, i):
                return (None, 16 * (t0 // 2 + 1) + 16 * i)

            def hi(c, dst, src, scale=1.0):
                act.wait_ge(s_mm, c + 1)
                act.activation(dst, src, ACT.Copy, scale=scale).then_inc(s_hi, 1)

            def sqrt_var(r, n):
                act.wait_ge(s_agg, n + 1)
                act.activation(sd[:, r:r + 1], mv[:, r, 1:2], ACT.Sqrt, bias=eps_ap).then_inc(s_sd, 1)

            def xt_hi(r, h, c):
                hi(c, XT[0][:, 4 * h:4 * h + 4, r * P:(r + 1) * P],
                   gb(c)[:, :].rearrange("p (k n) -> p k n", k=4))

            eps_ap = small[:, 208:209]
            act.wait_ge(s_link, 1)
            slab_hi(0, 0, 0)
            for r in range(RT + 1):
                if r < RT:
                    sqrt_var(r, r)
                if r >= 1:
                    for h in range(2):
                        xt_hi(r - 1, h, C_LN1 + 2 * (r - 1) + h)
            for j in range(6):
                act.wait_ge(s_piece[j % 3], 16 * (j // 3 + 1))
                act.activation(WKV[j][0], PRAW[j], ACT.Copy).then_inc(s_phi, 1)

            with act.Fori(0, NH // 2) as i:
                for s in range(2):
                    m = 2 * i + s
                    slab_hi(loads(T_Q + 2 * s, i), 1 - s, C_Q + 2 * m)
                    act.wait_ge(s_qst[s], FREE + 32 * i)
                    for h in range(2):
                        c = C_Q + 2 * s + h
                        hi(C_Q + 2 * m + h, QST[s][0][:, h * HALF:(h + 1) * HALF], gb(c)[:, 0:HALF], SCALE)

            for s in range(2):
                act.wait_ge(s_qst[s], FREE + 16 * 2 * NH // 2)
            for j in range(6, 8):
                act.wait_ge(s_piece[j - 3], 16)
                act.activation(WKV[j][0], PRAW[j], ACT.Copy).then_inc(s_phi, 1)

            def ctx_hi(b, j, c):
                act.wait_ge(s_ctx, 16 * (b + 1))
                act.wait_ge(s_mm, c)
                act.activation(HT[j][0][:, :, 0:SC], CRAW, ACT.Copy).then_inc(s_chi, 1)

            def kv_hi(b, j, before, more):
                if more:
                    ctx_hi(b + 1, 1 - j, C_KV + 8 * b)
                for u in range(8):
                    s, c = u % 2, C_KV + u
                    p, n = (P, KP) if u < 4 else (KT, 512)
                    act.wait_ge(s_kvst[s], FREE + before + [0, 0, 16, 16, 32, 32, 64, 64][u])
                    hi(C_KV + 8 * b + u, KVST[s][0][0:p, 0:n], gb(c)[0:p, 0:n])

            act.wait_ge(s_xt, 16 * 2 * B)
            ctx_hi(0, 0, C_KV)
            with act.Fori(0, B // 2 - 1) as i:
                for j in range(2):
                    kv_hi(2 * i + j, j, (2 * i + j) * 96, True)
            kv_hi(B - 2, 0, (B - 2) * 96, True)
            kv_hi(B - 1, 1, (B - 1) * 96, False)

            def exp(n, i):
                act.wait_ge(s_max, QT * n + i + 1)
                act.activation(PR[i][:, 0:KEYS], SB[i % 3][:, 0:KEYS], ACT.Exp, bias=negmax[:, i:i + 1],
                               accum_out=rowsum[:, i:i + 1]).then_inc(s_exp, 1)

            def attention(n, b, scores, av):
                for i in range(QT):
                    if av:
                        act.wait_ge(s_t, QT * (n - 1) + i + 1)
                        act.activation(PT[0][0:KT, :, i * P:(i + 1) * P],
                                       TB[i % 2][0:KT, :].rearrange("p (t n) -> p t n", t=4),
                                       ACT.Copy).then_inc(s_pth, 1)
                    if scores and i >= 1:
                        exp(n, i - 1)
                if scores:
                    exp(n, QT - 1)
                if av:
                    for a, (lo, up) in enumerate(((0, QA), (QA, QC))):
                        act.wait_ge(s_av, 2 * (n - 1) + a + 1)
                        act.activation(ATf[0][:, b, lo:up], AV[a][:, 0:up - lo], ACT.Copy).then_inc(s_avh, 1)

            def wo_slabs(kv):
                with act.Fori(0, NK // 2) as i:
                    for s in range(2):
                        slab_hi((None, 16 * (T_WO // 2 + 1 + s) + 16 * (kv * (NK // 2) + i)), 1 - s,
                                C_WO + kv * 2 * NK + 4 * i + 2 * s)

            act.wait_ge(s_zero, 2)
            attention(0, 0, True, False)
            with act.Fori(0, NKV - 1) as kv:
                with act.Fori(0, B) as b:
                    attention(kv * B + b + 1, b, True, True)
                wo_slabs(kv)
            with act.Fori(0, B - 1) as b:
                attention((NKV - 1) * B + b + 1, b, True, True)
            attention(NKV * B, B - 1, False, True)
            wo_slabs(NKV - 1)

            for g, (what, r, h) in enumerate(LN2_GROUPS):
                if what == "y" and h == 1:
                    sqrt_var(r, RT + r)
                if what == "n":
                    xt_hi(r, h, C_LN2 + g)

            def to_inner(c, j, h, dst):
                hi(c, dst[:, j, h * HALF:(h + 1) * HALF], gb(c)[:, 0:HALF])

            act.wait_ge(s_misc, 32)
            act.wait_ge(s_gz, 1)
            act.activation(GT[0][:, :, 0:NE], gate_raw[:, :].rearrange("p (k e) -> p k e", k=NK),
                           ACT.Copy).then_inc(s_phi, 1)
            for m in range(LAT // P):
                slab_hi(T_FC1 + m + 1, (m + 1) % 2, C_FC1 + 2 * m)
                for h in range(2):
                    to_inner(C_FC1 + 2 * m + h, m, h, IN[0])
            for m in range(LAT // P):
                if m % 2 == 0:
                    t = T_EXP + m // 2
                    slab_hi(t + 1, (t + 1) % 2, C_EXP + 2 * m)
                for h in range(2):
                    c = C_EXP + 2 * m + h
                    act.wait_ge(s_ev, c + 1)
                    act.activation(IN[0][:, 4 + m, h * HALF:(h + 1) * HALF], SQT, ACT.Copy).then_inc(s_hi, 1)
            for m in range(0, NK, 2):
                t = T_FC2 + m // 2
                slab_hi(t + 1, (t + 1) % 2, C_FC2 + 2 * m)

            def up_down(f, last):
                c0 = C_FFN + f * 4 * NK
                t0 = T_FFN // 2 + 1 + f * NK
                with act.Fori(0, NK // 2) as i:
                    for s in range(2):
                        m = 2 * i + s
                        slab_hi((None, 16 * (t0 + s) + 16 * i), 1 - s, c0 + 2 * m)
                        for h in range(2):
                            c = c0 + 2 * m + h
                            act.wait_ge(s_mm, c + 1)
                            act.activation(RELU, gb(C_FFN + 2 * s + h)[:, 0:HALF], ACT.Relu).then_inc(s_relu, 1)
                            act.wait_ge(s_ev, c + 1)
                            act.activation(IN[0][:, m, h * HALF:(h + 1) * HALF], SQT, ACT.Copy).then_inc(s_hi, 1)
                c0, t0 = c0 + 2 * NK, t0 + NK // 2
                for part_of in ((NK // 2 - 1, True), (1, not last)):
                    n, both = part_of
                    i0 = 0 if n > 1 else NK // 2 - 1
                    with act.Fori(i0, i0 + n) as i:
                        for s in range(2 if both else 1):
                            slab_hi((None, 16 * (t0 + s) + 16 * i), 1 - s, c0 + 4 * i + 2 * s)

            up_down(0, False)
            up_down(1, True)

            for r in range(RT):
                sqrt_var(r, 2 * RT + r)

        @block.vector
        def _(dve):
            chain = [0]

            def link(ins):
                chain[0] += 1
                ins.then_inc(s_link, 1)
                dve.wait_ge(s_link, chain[0])

            def lo(c, h, dst, src, hi_of):
                dve.wait_ge(s_hi, h + 1)
                dve.tensor_tensor(dst, src, f32(hi_of), ALU.subtract).then_inc(s_ev, 1)

            def xt_lo(r, h, c, nh):
                at = (slice(None), slice(4 * h, 4 * h + 4), slice(r * P, (r + 1) * P))
                lo(c, nh, XT[1][at], gb(c)[:, :].rearrange("p (k n) -> p k n", k=4), XT[0][at])

            def mean_var(r, n, halves):
                for h in range(2):
                    ins = dve.bn_stats(stats[:, 6 * h:6 * h + 6], halves[h])
                link(ins)
                dve.bn_aggr(mv[:, r, :], stats).then_inc(s_agg, 1)
                dve.wait_ge(s_agg, n + 1)

            def reciprocal_sd(r, n):
                dve.wait_ge(s_sd, n + 1)
                link(dve.reciprocal(rs[:, r:r + 1], sd[:, r:r + 1]))

            def normalise(r, n, dst, src):
                reciprocal_sd(r, n)
                dve.tensor_scalar(dst, src, mv[:, r, 0:1], rs[:, r:r + 1], ALU.subtract, ALU.mult).then_inc(s_xn, 1)

            link(dve.memset(small[:, 208:209], EPS))
            for r in range(RT + 2):
                if r < RT:
                    dve.wait_ge(s_x[r], 16)
                    mean_var(r, r, [X7[:, r, 0:512], X7[:, r, 512:1024]])
                if 1 <= r <= RT:
                    normalise(r - 1, r - 1, X7[:, r - 1, :], X7[:, r - 1, :])
                if r >= 2:
                    for h in range(2):
                        c = C_LN1 + 2 * (r - 2) + h
                        xt_lo(r - 2, h, c, H_LN1 + 2 * (r - 2) + h)

            def piece_lo(j):
                dve.wait_ge(s_phi, j + 1)
                dve.tensor_tensor(WKV[j][1], PRAW[j], f32(WKV[j][0]), ALU.subtract).then_inc(s_plo, 1)

            for j in range(6):
                piece_lo(j)

            with dve.Fori(0, NH // 2) as i:
                for s in range(2):
                    for h in range(2):
                        dve.wait_ge(s_hi, H_Q + 4 * i + 2 * s + h + 1)
                        cols = slice(h * HALF, (h + 1) * HALF)
                        dve.scalar_tensor_tensor(out=QST[s][1][:, cols], in0=gb(C_Q + 2 * s + h)[:, 0:HALF],
                                                 scalar=SCALE, in1=f32(QST[s][0][:, cols]),
                                                 op0=ALU.mult, op1=ALU.subtract).then_inc(s_ev, 1)
            for j in range(6, 8):
                piece_lo(j)

            with dve.Fori(0, B) as b:
                for u in range(8):
                    s = u % 2
                    p, n = (P, KP) if u < 4 else (KT, 512)
                    lo(None, H_KV + 8 * b + u, KVST[s][1][0:p, 0:n], gb(C_KV + u)[0:p, 0:n], KVST[s][0][0:p, 0:n])

            def reciprocal_sum(n, i):
                dve.wait_ge(s_exp, QT * n + i + 1)
                dve.reciprocal(rrow[:, i:i + 1], rowsum[:, i:i + 1]).then_inc(s_rec, 1)

            def attention(n, b, scores, av):
                for i in range(QT):
                    if av:
                        dve.wait_ge(s_pth, QT * (n - 1) + i + 1)
                        cols = slice(i * P, (i + 1) * P)
                        dve.tensor_tensor(PT[1][0:KT, :, cols], TB[i % 2][0:KT, :].rearrange("p (t n) -> p t n", t=4),
                                          f32(PT[0][0:KT, :, cols]), ALU.subtract).then_inc(s_ptl, 1)
                    if scores:
                        dve.wait_ge(s_s, QT * n + i + 1)
                        dve.reduce_max(negmax[:, i:i + 1], SB[i % 3][:, 0:KEYS], AX.X,
                                       negate=True).then_inc(s_max, 1)
                        if i >= 2:
                            reciprocal_sum(n, i - 2)
                if scores:
                    for i in range(QT - 2, QT):
                        reciprocal_sum(n, i)
                if av:
                    for a, (first, end) in enumerate(((0, QA), (QA, QC))):
                        dve.wait_ge(s_avh, 2 * (n - 1) + a + 1)
                        dve.tensor_tensor(ATf[1][:, b, first:end], AV[a][:, 0:end - first],
                                          f32(ATf[0][:, b, first:end]), ALU.subtract).then_inc(s_avl, 1)

            def add_to_y(c, c_static, m, h):
                dve.wait_ge(s_mm, c + 1)
                cols = slice(h * HALF, (h + 1) * HALF)
                dve.tensor_tensor(Y[:, m, cols], Y[:, m, cols], gb(c_static)[:, 0:HALF], ALU.add).then_inc(s_ev, 1)

            def y_slabs(c0, c_static):
                with dve.Fori(0, NK // 2) as i:
                    for s in range(2):
                        for h in range(2):
                            add_to_y(c0 + 4 * i + 2 * s + h, c_static + 2 * s + h, 2 * i + s, h)

            dve.wait_ge(s_zero, 2)
            attention(0, 0, True, False)
            with dve.Fori(0, NKV - 1) as kv:
                with dve.Fori(0, B) as b:
                    attention(kv * B + b + 1, b, True, True)
                y_slabs(C_WO + kv * 2 * NK, C_WO)
            with dve.Fori(0, B - 1) as b:
                attention((NKV - 1) * B + b + 1, b, True, True)
            attention(NKV * B, B - 1, False, True)
            y_slabs(C_WO + (NKV - 1) * 2 * NK, C_WO)

            nh = H_LN2
            for g, (what, r, h) in enumerate(LN2_GROUPS):
                c, cols = C_LN2 + g, slice(512 * h, 512 * h + 512)
                if what == "y":
                    dve.wait_ge(s_mm, c + 1)
                    if h == 0:
                        dve.wait_ge(s_xin[r % 2], 16 * (r // 2 + 1))
                    dve.tensor_tensor(XIN[r % 2][:, cols], XIN[r % 2][:, cols], gb(c)[:, :], ALU.add).then_inc(s_ev, 1)
                    if h == 1:
                        dve.wait_ge(s_ev, c + 1)
                        mean_var(r, RT + r, [XIN[r % 2][:, 0:512], XIN[r % 2][:, 512:1024]])
                        if r >= 1:
                            dve.wait_ge(s_mm, C_LN2 + 4 * r + 2)
                        normalise(r, RT + r, XN, XIN[r % 2])
                else:
                    xt_lo(r, h, c, nh)
                    nh += 1

            dve.wait_ge(s_phi, 9)
            dve.tensor_tensor(GT[1][:, :, 0:NE], gate_raw[:, :].rearrange("p (k e) -> p k e", k=NK),
                              f32(GT[0][:, :, 0:NE]), ALU.subtract).then_inc(s_gs, 1)

            def inner_lo(c, nh, m, h):
                cols = slice(h * HALF, (h + 1) * HALF)
                lo(c, nh, IN[1][:, m, cols], gb(c)[:, 0:HALF], IN[0][:, m, cols])

            for m in range(LAT // P):
                for h in range(2):
                    inner_lo(C_FC1 + 2 * m + h, H_FC1 + 2 * m + h, m, h)
            for s in range(2):
                dve.wait_ge(s_x2st[s], 16 * ((RT + 1 - s) // 2))
            for h in range(2):
                c = C_GATE + h
                dve.wait_ge(s_mm, c + 1)
                dve.tensor_copy(LGT[0:NE, h * HALF:(h + 1) * HALF], gb(c)[0:NE, 0:HALF]).then_inc(s_ev, 1)
            c = C_GATE + 2
            dve.wait_ge(s_mm, c + 1)
            dve.tensor_copy(lg, gb(c)[:, 0:RT * NE]).then_inc(s_ev, 1)
            dve.wait_ge(s_ev, c + 1)
            for r in range(RT):
                ins = dve.max(top8[:, r * NE:(r + 1) * NE], lg[:, r * NE:(r + 1) * NE])
            link(ins)
            best = top8.rearrange("p (r e) -> p r e", e=NE)
            link(dve.tensor_tensor(rw.rearrange("p (r e) -> p r e", e=1), best[:, :, 0:1], best[:, :, 1:2], ALU.add))
            for r in range(RT):
                dve.tensor_scalar(RWREP[:, r, :], ones[:, :], rw[:, r:r + 1], None, ALU.mult).then_inc(s_rw, 1)
            for a, (first, end) in enumerate(((0, QA), (QA, QC))):
                dve.wait_ge(s_mm, C_GATE + 4 + a)
                dve.tensor_copy(RWB[:, first:end], gb(C_GATE + 3 + a)[:, 0:end - first]).then_inc(s_ev, 1)
            dve.wait_ge(s_ev, C_EXP)

            for m in range(LAT // P):
                for h in range(2):
                    c, cols = C_EXP + 2 * m + h, slice(h * HALF, (h + 1) * HALF)
                    dve.wait_ge(s_mm, c + 1)
                    dve.wait_ge(s_lo, L_EXP + 2 * m + h)
                    dve.tensor_tensor(SQT, gb(c)[:, 0:HALF], RWB[:, cols], ALU.mult).then_inc(s_ev, 1)
                    dve.wait_ge(s_hi, H_EXP + 2 * m + h + 1)
                    dve.tensor_tensor(IN[1][:, 4 + m, cols], SQT, f32(IN[0][:, 4 + m, cols]),
                                      ALU.subtract).then_inc(s_lo, 1)
            for m in range(NK):
                for h in range(2):
                    c = C_FC2 + 2 * m + h
                    dve.wait_ge(s_mm, c + 1)
                    dve.tensor_copy(Y[:, m, h * HALF:(h + 1) * HALF], gb(c)[:, 0:HALF]).then_inc(s_ev, 1)

            with dve.Fori(0, 2) as f:
                with dve.Fori(0, NK // 2) as i:
                    for s in range(2):
                        for h in range(2):
                            n = f * 2 * NK + 4 * i + 2 * s + h
                            cols = slice(h * HALF, (h + 1) * HALF)
                            dve.wait_ge(s_lo, L_FFN + n)
                            dve.wait_ge(s_relu, n + 1)
                            dve.scalar_tensor_tensor(out=SQT, in0=gb(C_FFN + 2 * s + h)[:, 0:HALF], scalar=0.0,
                                                     in1=RELU, op0=ALU.max, op1=ALU.mult).then_inc(s_ev, 1)
                            dve.wait_ge(s_hi, H_FFN + n + 1)
                            dve.tensor_tensor(IN[1][:, 2 * i + s, cols], SQT, f32(IN[0][:, 2 * i + s, cols]),
                                              ALU.subtract).then_inc(s_lo, 1)
                y_slabs(C_FFN + 2 * NK + f * 4 * NK, C_FFN)

            dve.wait_ge(s_gamma, 16)
            for r in range(RT):
                s, c = r % 2, C_LN3 + 2 * r
                dve.wait_ge(s_mm, c + 2)
                mean_var(r, 2 * RT + r, [gb(c)[:, :], gb(c + 1)[:, :]])
                reciprocal_sd(r, 2 * RT + r)
                for h in range(2):
                    cols = slice(512 * h, 512 * h + 512)
                    ins = dve.scalar_tensor_tensor(out=CEN[:, cols], in0=gb(c + h)[:, :], scalar=mv[:, r, 0:1],
                                                   in1=GAMMA[:, cols], op0=ALU.subtract, op1=ALU.mult)
                    ins.then_inc(s_ev, 1)
                dve.wait_ge(s_ev, c + 2)
                dve.wait_ge(s_xin[s], 16 * ((RT + 1 - s) // 2 + r // 2 + 1))
                dve.scalar_tensor_tensor(out=XB[s], in0=CEN, scalar=rs[:, r:r + 1], in1=XB[s],
                                         op0=ALU.mult, op1=ALU.add).then_inc(s_o, 1)

        @block.tensor
        def _(pe):
            def bank_free(c):
                pe.wait_ge(s_ev, c - 3)

            def three(out_ap, w, a, first, last):
                pe.matmul(out_ap, w[0], a[0], start=first, stop=False)
                pe.matmul(out_ap, w[0], a[1], start=False, stop=False)
                return pe.matmul(out_ap, w[1], a[0], start=False, stop=last)

            def slab_tile(s, act_hl, cols, k0, nk, w0, c, c_static):
                bank_free(c)
                for k in range(nk):
                    w = [WS[s][l][:, (w0 + k) * P:(w0 + k + 1) * P] for l in range(2)]
                    last = three(cols(gb(c_static)), w, [act_hl(l, k0 + k) for l in range(2)], k == 0, k == nk - 1)
                last.then_inc(s_mm, 1)

            def half_of(tiles, h):
                return lambda l, k: tiles[l][:, k, h * HALF:(h + 1) * HALF]

            def whole(b_):
                return b_[:, 0:HALF]

            def transposes(c, src):
                if c >= 4:
                    bank_free(c)
                for k in range(4):
                    last = pe.transpose(gb(c)[:, k * P:(k + 1) * P], src(k), ident[:, :])
                last.then_inc(s_mm, 1)

            pe.wait_ge(s_const, 3)
            for r in range(RT):
                pe.wait_ge(s_xn, r + 1)
                for h in range(2):
                    transposes(C_LN1 + 2 * r + h, lambda k: X7[:, r, (4 * h + k) * P:(4 * h + k + 1) * P])

            pe.wait_ge(s_ev, C_Q)
            with pe.Fori(0, NH // 2) as i:
                for s in range(2):
                    m = 2 * i + s
                    pe.wait_ge(s_wlo, T_Q + m + 1)
                    for h in range(2):
                        slab_tile(s, half_of(XT, h), whole, 0, NK, 0, C_Q + 2 * m + h, C_Q + 2 * s + h)

            pe.wait_ge(s_plo, 8)
            pe.wait_ge(s_pad, 4)

            def wkv(which, k, l, first, n):
                return WKV[which * 4 + k // 2][l][:, (k % 2) * 512 + first:(k % 2) * 512 + first + n]

            with pe.Fori(0, B // 2) as i:
                for j in range(2):
                    b = 2 * i + j
                    pe.wait_ge(s_clo, b + 1)
                    pe.wait_ge(s_lat[j], 32 * (i + 1))
                    for u in range(8):
                        bank_free(C_KV + 8 * b + u)
                        dst = gb(C_KV + u)
                        for k in range(NK):
                            if u < 4:
                                last = three(dst[:, 0:KP], [wkv(0, k, l, u * D, D) for l in range(2)],
                                             [HT[j][l][:, k, :] for l in range(2)], k == 0, k == NK - 1)
                            else:
                                last = three(dst[0:KT, :], [HT[j][l][:, k, (u - 4) * KT:(u - 3) * KT] for l in range(2)],
                                             [wkv(1, k, l, 0, 512) for l in range(2)], k == 0, k == NK - 1)
                        last.then_inc(s_mm, 1)

            def av(s, a, ts):
                first, end = ((0, QA), (QA, QC))[a]
                for t in ts:
                    last = three(AV[a][:, 0:end - first],
                                 [VB[s][0:KT, (l * 4 + t) * D:(l * 4 + t + 1) * D] for l in range(2)],
                                 [PT[l][0:KT, t, first:end] for l in range(2)], t == 0, t == 3)
                return last

            def attention(n, s, loads, scores, with_av):
                for i in range(QT):
                    if with_av:
                        pe.wait_ge(s_pn, QT * (n - 1) + i + 1)
                        if i >= 2:
                            pe.wait_ge(s_ptl, QT * (n - 1) + i - 1)
                        for t in range(4):
                            last = pe.transpose(TB[i % 2][0:KT, t * P:(t + 1) * P], PR[i][:, t * KT:(t + 1) * KT],
                                                ident[:, :])
                        last.then_inc(s_t, 1)
                    if scores:
                        if i == 0:
                            pe.wait_ge(s_qk[s], loads)
                        if i >= 3 or with_av:
                            pe.wait_ge(s_exp, QT * n + max(i - 2, 0))
                        three(SB[i % 3][:, 0:KP], [QB[s][:, l * QC + i * P:l * QC + (i + 1) * P] for l in range(2)],
                              [KB[s][:, l * KP:(l + 1) * KP] for l in range(2)], True, True).then_inc(s_s, 1)
                    if with_av:
                        if i == 4:
                            pe.wait_ge(s_v[1 - s], loads_of_v(n, s))
                            pe.wait_ge(s_ptl, QT * (n - 1) + 4)
                            pe.wait_ge(s_avl, 1 + 2 * (n - 1))
                            av(1 - s, 0, [0])
                        if i == 5:
                            av(1 - s, 0, [1, 2])
                        if i == 6:
                            av(1 - s, 0, [3]).then_inc(s_av, 1)
                            pe.wait_ge(s_ptl, QT * n)
                            av(1 - s, 1, range(4)).then_inc(s_av, 1)

            def loads_of_v(n, s):
                return 8 * (n + 1) if s == 1 else 8 * n

            def loads_of_qk(n, s):
                return 16 * (n + 1) if s == 1 else 16 * (n + 2)

            def wo_slabs(kv):
                with pe.Fori(0, NK // 2) as i:
                    pe.wait_ge(s_avl, 1 + 2 * B * (kv + 1))
                    for s in range(2):
                        m = 2 * i + s
                        pe.wait_ge(s_wlo, T_WO + kv * NK + m + 1)
                        for h in range(2):
                            slab_tile(s, lambda l, k: AT[l][:, 4 * h:4 * h + 4, k, :],
                                      lambda b_: b_[:, 0:HALF].rearrange("p (b s) -> p b s", b=4),
                                      0, G, 0, C_WO + kv * 2 * NK + 2 * m + h, C_WO + 2 * s + h)

            pe.wait_ge(s_ev, C_WO)
            attention(0, 0, 32, True, False)
            with pe.Fori(0, NKV - 1) as kv:
                with pe.Fori(0, B // 2) as i:
                    pe.wait_ge(s_ev, C_WO + kv * 2 * NK)
                    for j in range(2):
                        n = kv * B + 2 * i + j + 1
                        attention(n, 1 - j, loads_of_qk(n, 1 - j), True, True)
                wo_slabs(kv)
            pe.wait_ge(s_ev, C_WO + (NKV - 1) * 2 * NK)
            with pe.Fori(0, B // 2 - 1) as i:
                for j in range(2):
                    n = (NKV - 1) * B + 2 * i + j + 1
                    attention(n, 1 - j, loads_of_qk(n, 1 - j), True, True)
            n = NKV * B - 1
            attention(n, 1, loads_of_qk(n, 1), True, True)
            attention(n + 1, 0, 0, False, True)
            wo_slabs(NKV - 1)

            pe.wait_ge(s_ev, C_LN2)
            for g, (what, r, h) in enumerate(LN2_GROUPS):
                if what == "y":
                    transposes(C_LN2 + g, lambda k: Y[:, 4 * h + k, r * P:(r + 1) * P])
                else:
                    pe.wait_ge(s_xn, RT + r + 1)
                    transposes(C_LN2 + g, lambda k: XN[:, (4 * h + k) * P:(4 * h + k + 1) * P])

            pe.wait_ge(s_ev, C_FC1)
            for m in range(LAT // P):
                pe.wait_ge(s_wlo, T_FC1 + m + 1)
                for h in range(2):
                    c = C_FC1 + 2 * m + h
                    slab_tile(m % 2, half_of(XT, h), whole, 0, NK, 0, c, c)
            pe.wait_ge(s_gs, 1)
            for h in range(2):
                c = C_GATE + h
                bank_free(c)
                for k in range(NK):
                    last = three(gb(c)[:, 0:HALF], [GT[l][:, k, :] for l in range(2)],
                                 [XT[l][:, k, h * HALF:(h + 1) * HALF] for l in range(2)], k == 0, k == NK - 1)
                last.then_inc(s_mm, 1)
            c = C_GATE + 2
            pe.wait_ge(s_ev, C_GATE + 2)
            for r in range(RT):
                last = pe.transpose(gb(c)[:, r * NE:(r + 1) * NE], LGT[0:NE, r * P:(r + 1) * P], ident[0:NE, 0:NE])
            last.then_inc(s_mm, 1)
            pe.wait_ge(s_rw, RT)
            for a, tiles in enumerate((range(0, 4), range(4, RT))):
                c = C_GATE + 3 + a
                bank_free(c)
                for r in tiles:
                    last = pe.transpose(gb(c)[:, (r % 4) * P:(r % 4 + 1) * P], RWREP[:, r, :], ident[:, :])
                last.then_inc(s_mm, 1)
            for m in range(LAT // P):
                t = T_EXP + m // 2
                pe.wait_ge(s_wlo, t + 1)
                for h in range(2):
                    c = C_EXP + 2 * m + h
                    slab_tile(t % 2, half_of(IN, h), whole, 0, 4, 4 * (m % 2), c, c)
            pe.wait_ge(s_lo, L_FFN)
            for m in range(NK):
                t = T_FC2 + m // 2
                pe.wait_ge(s_wlo, t + 1)
                for h in range(2):
                    c = C_FC2 + 2 * m + h
                    slab_tile(t % 2, half_of(IN, h), whole, 4, 4, 4 * (m % 2), c, c)
            with pe.Fori(0, 2) as f:
                for n, tiles in enumerate((XT, IN)):
                    with pe.Fori(0, NK // 2) as i:
                        if n == 1:
                            pe.wait_ge(s_lo, L_FFN + 2 * NK * (f + 1))
                        for s in range(2):
                            m = 2 * i + s
                            pe.wait_ge(s_wlo, T_FFN + (2 * f + n) * NK + m + 1)
                            for h in range(2):
                                slab_tile(s, half_of(tiles, h), whole, 0, NK, 0,
                                          C_FFN + (2 * f + n) * 2 * NK + 2 * m + h, C_FFN + 2 * s + h)

            pe.wait_ge(s_ev, C_LN3)
            for r in range(RT):
                for h in range(2):
                    transposes(C_LN3 + 2 * r + h, lambda k: Y[:, 4 * h + k, r * P:(r + 1) * P])


def kernel(x, ctx_4096, L0_xattn_Wq, L0_xattn_Wk, L0_xattn_Wv, L0_xattn_Wo, L0_ffn_gate_w, L0_ffn_up_w,
           L0_ffn_down_w, L0_ffn_fc1_w, L0_ffn_fc2_w, L0_ffn_expert_w, L0_ffn_ln_gamma, L0_ffn_ln_beta):
    import numpy as np
    import concourse.bacc as bacc
    from concourse import mybir as mb
    from concourse.bass_utils import run_bass_kernel_spmd

    def tiles(w, nk, per):
        w = np.asarray(w)
        k, m = w.shape
        a = w.reshape(k // (nk * P), nk, P, m // (per * P), per, P)
        return a.transpose(0, 3, 2, 4, 1, 5).reshape(-1, P, per * nk * P)

    up, down = np.asarray(L0_ffn_up_w), np.asarray(L0_ffn_down_w)
    slabs = np.concatenate([
        tiles(L0_xattn_Wq, NK, 1), tiles(L0_xattn_Wo, G, 1), tiles(L0_ffn_fc1_w, NK, 1),
        tiles(L0_ffn_expert_w, 4, 2), tiles(L0_ffn_fc2_w, 4, 2),
        tiles(up[:, 0:1024], NK, 1), tiles(down[0:1024], NK, 1),
        tiles(up[:, 1024:2048], NK, 1), tiles(down[1024:2048], NK, 1)])
    wkv = np.concatenate([np.asarray(w).reshape(4, 2, P, 512).transpose(0, 2, 1, 3).reshape(4, P, 1024)
                          for w in (L0_xattn_Wk, L0_xattn_Wv)])
    ctxT = np.asarray(ctx_4096).reshape(B, SC, NK, P).transpose(0, 3, 2, 1)
    gate = np.asarray(L0_ffn_gate_w).reshape(NK, P, NE).transpose(1, 0, 2).reshape(P, NK * NE)
    laid = {"x": np.asarray(x).reshape(ROWS, HID), "ctxT": ctxT, "slabs": slabs, "wkv": wkv, "gate": gate,
            "gamma": L0_ffn_ln_gamma, "beta": L0_ffn_ln_beta}

    nc = bacc.Bacc("TRN2", target_bir_lowering=False, num_devices=1)
    arrays, args = {}, []
    for name, a in laid.items():
        a = np.ascontiguousarray(a)
        arrays[f"in_{name}"] = a
        args.append(nc.dram_tensor(f"in_{name}", a.shape, mb.dt.from_np(a.dtype), kind="ExternalInput").ap())
    args.append(nc.dram_tensor("out", (ROWS, HID), mb.dt.float32, kind="ExternalOutput").ap())
    xattn_ffn(nc, *args)
    r = run_bass_kernel_spmd(nc, [arrays], core_ids=[0])
    return r.results[0]["out"].reshape(B, SQ, HID)
```

```python
from contextlib import ExitStack

import concourse.bass as bass
from concourse import mybir

F32 = mybir.dt.float32
F32R = mybir.dt.float32r
ALU = mybir.AluOpType
ACT = mybir.ActivationFunctionType
AX = mybir.AxisListType

P = 128
B, SQ, HID = 8, 112, 1024
SC = 375
NH, NKV, D = 32, 4, 128
G = NH // NKV
INT, LAT, NE = 2048, 512, 8
KEYS = SC + SQ
KP = 488
KT = KP // 4
ROWS = B * SQ
RT = ROWS // P
PARTS = ((0, 4 * P), (4 * P, ROWS))
NK = HID // P
QC = G * SQ
QT = QC // P
QH = QC // 2
SLAB = NK * P
SCALE = float(D) ** -0.5
FREE = 16
EPS = 1e-5

T_Q = 0
T_WO = T_Q + NH
T_FC1 = T_WO + NKV * NK
T_EXP = T_FC1 + LAT // P
T_FC2 = T_EXP + LAT // P // 2
T_FFN = T_FC2 + HID // P // 2
N_SLABS = T_FFN + 4 * NK

EDGE = 4
SLAB_AT = (2 * list(range(EDGE)) + list(range(EDGE, NH - EDGE)) + 2 * list(range(NH - EDGE, NH))
           + list(range(T_WO, T_FC1)) + list(range(T_FC1 - NK, T_FC1))
           + 2 * list(range(T_FC1, T_EXP)) + list(range(T_EXP, N_SLABS)) + list(range(N_SLABS - NK, N_SLABS)))
P_Q2 = 2 * EDGE
P_Q3 = P_Q2 + NH - 2 * EDGE
P_WO = P_Q3 + 2 * EDGE
P_SEG2 = P_WO + (NKV - 1) * NK
P_FC1 = P_SEG2 + 2 * NK
P_EXP = P_FC1 + 2 * (LAT // P)
P_FC2 = P_EXP + LAT // P // 2
P_FFN = P_FC2 + HID // P // 2
P_SEG3 = P_FFN + 3 * NK
N_POS = P_SEG3 + 2 * NK
assert N_POS == len(SLAB_AT)


def both(what, r):
    return [(what, r, 0), (what, r, 1)]


def weave(products, between):
    return [g for j, p in enumerate(products) for g in [p] + between.get(j, [])]


SEG1 = [g for r in range(4) for g in both("ln", r)] + weave(
    [("q", h * EDGE + m, m, h) for h in range(2) for m in range(EDGE)], {j: both("ln", 4 + j) for j in range(3)})
SEG_Q3 = [("q", P_Q3 + h * EDGE + m, NH - EDGE + m, h) for h in range(2) for m in range(EDGE)]
SEG2 = [("wo", P_SEG2 + m, m, 0) for m in range(NK)] + weave(
    [("wo", P_SEG2 + NK + m, m, 1) for m in range(NK)],
    {0: both("y", 0), 1: both("n", 0) + both("y", 1), 2: both("n", 1) + both("y", 2),
     3: both("n", 2) + both("y", 3), 4: both("n", 3)}) + weave(
    [("fc1", P_FC1 + m, m, 0) for m in range(4)],
    {0: both("y", 4), 1: both("n", 4) + both("y", 5), 2: both("n", 5) + both("y", 6), 3: both("n", 6)}) + [
    ("logit", 0, 0, 0), ("logit", 0, 0, 1)] + weave(
    [("fc1", P_FC1 + 4 + m, m, 1) for m in range(4)],
    {0: [("logitT",)], 2: [("routing", 0), ("routing", 1)]}) + [
    ("exp", P_EXP + m // 2, m, h) for m in range(4) for h in range(2)] + [
    ("fc2", P_FC2 + m // 2, m, h) for m in range(NK) for h in range(2)]
SEG3 = [("down", P_SEG3 + m, m, 0) for m in range(NK)] + weave(
    [("down", P_SEG3 + NK + m, m, 1) for m in range(NK)],
    {0: both("z", 0), 1: both("z", 1), 2: both("z", 2), 3: both("z", 3)}) + [
    g for r in range(4, RT) for g in both("z", r)]

C_SEG1 = 0
C_Q2 = C_SEG1 + len(SEG1)
C_Q3 = C_Q2 + 2 * (NH - 2 * EDGE)
C_KV = C_Q3 + len(SEG_Q3)
C_WO = C_KV + 8 * B
C_SEG2 = C_WO + (NKV - 1) * 2 * NK
C_FFN = C_SEG2 + len(SEG2)
C_SEG3 = C_FFN + 3 * 2 * NK

WITH_HI = ("ln", "q", "n", "fc1", "exp")


def hi_before(segment, start):
    out = [start]
    for g in segment:
        out.append(out[-1] + (g[0] in WITH_HI))
    return out


H_SEG1 = hi_before(SEG1, 0)
H_Q2 = H_SEG1[-1]
H_Q3 = hi_before(SEG_Q3, H_Q2 + 2 * (NH - 2 * EDGE))
H_KV = H_Q3[-1]
H_SEG2 = hi_before(SEG2, H_KV + 8 * B)
H_FFN = H_SEG2[-1]
L_FFN = 2 * (LAT // P)


def xattn_ffn(nc, x, ctxT, slabs, wkv, gate, gamma, beta, out):
    with ExitStack() as top:
        def sb(name, cols, dt=F32):
            return top.enter_context(nc.sbuf_tensor(name, [P, cols], dt))

        def sem(name):
            return top.enter_context(nc.semaphore(name))

        def sems(name, n):
            return [sem(f"{name}{j}") for j in range(n)]

        def dram(name, shape):
            return nc.dram_tensor(name, shape, F32).ap()

        xt_d = dram("xt_scratch", (P, 2, NK, ROWS))
        q_d = dram("q_scratch", (NKV, P, 2, G, ROWS))
        k_d = dram("k_scratch", (NKV, B, P, 2 * KP))
        v_d = dram("v_scratch", (NKV, B, KT, 2, 4, D))
        k_f = k_d.rearrange("h b p c -> (h b) p c")
        v_f = v_d.rearrange("h b p l t d -> (h b) p (l t d)")
        x2_d = dram("x2_beta_scratch", (ROWS, HID))

        RA = sb("act_region", 2 * 2 * NK * KP, F32R)
        RB = sb("mid_region", 16384, F32R)
        RC = sb("slab_split", 4 * SLAB, F32R)
        RD = sb("small_region", 2048, F32R)
        RAW = sb("slab_raw", 2 * SLAB)
        FB = sb("tile_region", 4096)
        YR = sb("y_region", NK * ROWS)
        ident = sb("ident", P)
        ones = sb("ones", P)
        gate_raw = sb("gate_raw", NK * NE)
        small = sb("small", 224)

        def part(t, at, n):
            return t[:, at:at + n]

        def rows_hl(region, tiles):
            views, at_ = [], 0
            for first, end in PARTS:
                n = tiles * (end - first)
                views.append([part(region, at_ + l * n, n).rearrange("p (k n) -> p k n", k=tiles) for l in range(2)])
                at_ += 2 * n
            return views

        XT = rows_hl(RA, NK)
        AT = [part(RA, l * NK * ROWS, NK * ROWS).rearrange("p (g n) -> p g n", g=G) for l in range(2)]
        HT = [[part(RA, (2 * j + l) * NK * KP, NK * KP).rearrange("p (k n) -> p k n", k=NK)
               for l in range(2)] for j in range(2)]
        IN = rows_hl(RA, NK)
        PIECE = 2 * 512
        WKV = [[part(RB, (2 * j + l) * PIECE, PIECE) for l in range(2)] for j in range(8)]
        at = 0
        QB = [part(RB, at + s * 2 * QC, 2 * QC) for s in range(2)]
        at += 4 * QC
        KB = [part(RB, at + s * 2 * KP, 2 * KP) for s in range(2)]
        at += 4 * KP
        VB = [part(RB, at + s * 8 * D, 8 * D) for s in range(2)]
        assert at + 16 * D <= 8 * PIECE
        PT = [part(RB, 8 * PIECE + l * 4 * QC, 4 * QC).rearrange("p (t n) -> p t n", t=4) for l in range(2)]
        X2 = rows_hl(RB, NK)
        WS = [[part(RC, (2 * s + l) * SLAB, SLAB) for l in range(2)] for s in range(2)]
        KVST = [[part(RD, (2 * s + l) * 512, 512) for l in range(2)] for s in range(2)]
        QSTV = [part(RD, s * 1024, 1024).rearrange("p (l n) -> p l n", l=2) for s in range(2)]
        KVSTV = QSTV
        GT = [part(RD, l * NK * P, NK * P).rearrange("p (k n) -> p k n", k=NK) for l in range(2)]
        RAWS = [part(RAW, s * SLAB, SLAB) for s in range(2)]
        PRAW = [part(FB, (j % 3) * PIECE, PIECE) for j in range(8)]
        CRAW = part(FB, 0, NK * SC).rearrange("p (k n) -> p k n", k=NK)
        PR = [part(FB, i * KP, KP) for i in range(QT)]
        XIN = [part(FB, s * HID, HID) for s in range(2)]
        XN = part(FB, 2 * HID, HID)
        BETA = part(FB, 3 * HID, HID)
        RWREP = part(FB, 0, ROWS).rearrange("p (r n) -> p r n", r=RT)
        RWB = part(FB, HID, ROWS)
        LGT = part(FB, 2 * HID, ROWS)
        RELU = part(FB, 3 * HID, 512)
        SQT = part(FB, 3 * HID + 512, 512)
        GAMMA = part(FB, 0, HID)
        XB = [part(FB, (1 + s) * HID, HID) for s in range(2)]
        CEN = part(FB, 3 * HID, HID)
        X7 = YR[:, :].rearrange("p (r n) -> p r n", r=RT)
        Y = YR[:, :].rearrange("p (k n) -> p k n", k=NK)
        stats = small[:, 0:12]
        mv = small[:, 16:16 + 2 * RT].rearrange("p (r c) -> p r c", c=2)
        sd = small[:, 32:32 + RT]
        rs = small[:, 40:40 + RT]
        negmax = small[:, 48:48 + QT]
        rowsum = small[:, 56:56 + QT]
        rrow = small[:, 64:64 + QT]
        rw = small[:, 72:72 + RT]
        lg = small[:, 80:80 + RT * NE]
        top8 = small[:, 144:144 + RT * NE]

        bank = [top.enter_context(nc.psum_tensor(f"bank{j}", [P, 512], F32)) for j in range(8)]
        GB = [bank[7], bank[3], bank[4], bank[5]]
        SB, AV = bank[0:3], bank[5:7]
        order = [GB[(C_WO + j) % 4] for j in range(4)]
        LAST_USE = [j for j in range(4) if order[j] is not bank[5]]
        TB = [order[j] for j in LAST_USE]
        LAST_USE.append([j for j in range(4) if order[j] is bank[5]][0])

        def gb(c):
            return GB[c % 4]

        s_x = sems("x_loaded", RT)
        s_raw = sems("slab_loaded", 2)
        s_piece = sems("kv_piece_loaded", 3)
        s_ctx = sem("ctx_loaded")
        s_lat = sems("latents_loaded", 2)
        s_xt = sem("xt_stored")
        s_qst = sems("q_stored", 2)
        s_kvst = sems("kv_stored", 2)
        s_qk = sems("qk_loaded", 2)
        s_v = sems("v_loaded", 2)
        s_xin = sems("x_again", 2)
        s_x2st = sems("x2_stored", 2)
        s_misc = sem("gate_beta_loaded")
        s_gamma = sem("gamma_loaded")
        s_out = sems("out_stored", 2)
        s_const = sem("consts_made")
        s_agg = sem("stats_done")
        s_sd = sem("sd_done")
        s_link = sem("vector_chain")
        s_xn = sem("rows_normalised")
        s_mm = sem("group_done")
        s_hi = sem("hi_of_group")
        s_ev = sem("group_taken")
        s_lo = sem("lo_of_tile")
        s_relu = sem("relu_done")
        s_whi = sem("slab_hi")
        s_wlo = sem("slab_lo")
        s_phi = sem("piece_hi")
        s_plo = sem("piece_lo")
        s_chi = sem("ctx_hi")
        s_clo = sem("ctx_lo")
        s_pad = sem("pad_zeroed")
        s_s = sem("scores_done")
        s_max = sem("max_done")
        s_exp = sem("exp_done")
        s_rec = sem("reciprocal_done")
        s_pn = sem("p_normalised")
        s_t = sem("pT_done")
        s_pth = sem("pT_hi")
        s_ptl = sem("pT_lo")
        s_av = sem("av_done")
        s_avh = sem("av_hi")
        s_avl = sem("av_lo")
        s_zero = sem("y_zeroed")
        s_gz = sem("gate_zeroed")
        s_gs = sem("gate_split")
        s_x2 = sem("x2_summed")
        s_x2b = sem("x2_beta")
        s_rw = sem("routing_weight")
        s_o = sem("out_tile")

        top.enter_context(nc.allow_non_contiguous_dma(reason="scratch rows of 448 bytes"))
        block = top.enter_context(nc.Block())

        def f32(ap):
            return ap.bitcast(F32)

        def row_tile(xt, l, r, h):
            return xt[r // 4][l][:, 4 * h:4 * h + 4, (r % 4) * P:(r % 4 + 1) * P]

        @block.sync
        def _(sp):
            def load_slab(p, s, slab):
                sp.wait_ge(s_wlo, p - 1)
                sp.dma_start(RAWS[s], slabs[slab]).then_inc(s_raw[s], 16)

            def next_slab(p):
                if p + 2 < N_POS:
                    load_slab(p + 2, p % 2, SLAB_AT[p + 2])

            def next_slabs(p0, n):
                assert SLAB_AT[p0 + 2:p0 + n + 2] == list(range(SLAB_AT[p0 + 2], SLAB_AT[p0 + 2] + n))
                with sp.Fori(0, n // 2) as i:
                    for s in range(2):
                        load_slab(p0 + 2 + 2 * i + s, s, SLAB_AT[p0 + 2] + 2 * i + s)

            def load_piece(j):
                if j >= 3:
                    sp.wait_ge(s_plo, j - 2)
                sp.dma_start(PRAW[j], wkv[j]).then_inc(s_piece[j % 3], 16)

            for r in range(RT):
                sp.dma_start(X7[:, r, :], x[r * P:(r + 1) * P, :]).then_inc(s_x[r], 16)
                if r in (3, 5):
                    s = (r - 3) // 2
                    sp.dma_start(RAWS[s], slabs[s]).then_inc(s_raw[s], 16)
            for j in range(3):
                load_piece(j)

            def store_q(kv, g, h, c, slot):
                sp.wait_ge(s_ev, c + 1)
                first, end = PARTS[h]
                sp.dma_start(q_d[kv, :, :, g, first:end],
                             f32(QSTV[slot][:, :, 0:end - first])).then_inc(s_qst[slot], 16)

            def store_q_of(segment, c0, p):
                for j, g in enumerate(segment):
                    if g[0] == "q" and g[1] == p:
                        store_q(g[2] // G, g[2] % G, g[3], c0 + j, g[1] % 2)

            pieces = {3: (3, 4), 4: (5, 6), 5: (7,)}
            for p in range(2 * EDGE):
                next_slab(p)
                for j in pieces.get(p, ()):
                    load_piece(j)
                store_q_of(SEG1, C_SEG1, p)
            sp.wait_ge(s_plo, 8)
            sp.dma_start(CRAW, ctxT[0]).then_inc(s_ctx, 16)

            def q_position(p, s, m_hi, m_lo, c):
                load_slab(p + 2, s, p + 2 - EDGE)
                for h in range(2):
                    store_q(m_hi, m_lo, h, c + h, h)

            def q_heads(kv, first, n):
                for g in range(first, first + n):
                    m = kv * G + g
                    q_position(m + EDGE, g % 2, kv, g, C_Q2 + 2 * (m - EDGE))

            q_heads(0, EDGE, G - EDGE)
            with sp.Fori(1, NKV - 1) as kv:
                q_heads(kv, 0, G)
            q_heads(NKV - 1, 0, EDGE - 2)
            for g in range(EDGE - 2, G - EDGE):
                m = (NKV - 1) * G + g
                next_slab(m + EDGE)
                for h in range(2):
                    store_q(NKV - 1, g, h, C_Q2 + 2 * (m - EDGE) + h, h)

            def latents(b, j):
                for l in range(2):
                    sp.dma_start(f32(HT[j][l][:, :, SC:KEYS]), xt_d[:, l, :, bass.ds(b * SQ, SQ)]).then_inc(s_lat[j], 16)

            for p in range(P_Q3, P_WO):
                next_slab(p)
                if p == P_Q3 + EDGE:
                    sp.wait_ge(s_mm, C_Q3 + EDGE)
                    sp.wait_ge(s_xt, 16 * 4)
                    latents(0, 0)
                store_q_of(SEG_Q3, C_Q3, p)

            def kv_batch(b, j, more):
                if more:
                    sp.wait_ge(s_mm, C_KV + 8 * b)
                    latents(b + 1, 1 - j)
                    sp.wait_ge(s_clo, b + 1)
                    sp.dma_start(CRAW, ctxT[b + 1]).then_inc(s_ctx, 16)
                for u in range(8):
                    s = u % 2
                    sp.wait_ge(s_ev, C_KV + 8 * b + u + 1)
                    if u < 4:
                        sp.dma_start(k_d[u, b].rearrange("p (l c) -> p l c", l=2),
                                     f32(KVSTV[s][:, :, 0:KP])).then_inc(s_kvst[s], 16)
                    else:
                        for l in range(2):
                            sp.dma_start(v_d[:, b, :, l, u - 4, :].rearrange("h p d -> p h d"),
                                         f32(KVST[s][l])[0:KT, :].rearrange("p (h d) -> p h d", h=NKV)
                                         ).then_inc(s_kvst[s], 16)

            def load_qk(kv, b, n, s):
                for l in range(2):
                    sp.dma_start(f32(QB[s])[:, l * QC:(l + 1) * QC].rearrange("p (g c) -> p g c", g=G),
                                 q_d[kv, :, l, :, bass.ds(b * SQ, SQ)]).then_inc(s_qk[s], 16)
                sp.dma_start(f32(KB[s]), k_f[n]).then_inc(s_qk[s], 16)

            def load_v(n, s):
                sp.dma_start(f32(VB[s])[0:KT, :], v_f[n]).then_inc(s_v[s], 16)

            with sp.Fori(0, B // 2 - 1) as i:
                for j in range(2):
                    kv_batch(2 * i + j, j, True)
            kv_batch(B - 2, 0, True)
            for s in range(2):
                sp.wait_ge(s_qst[s], FREE + 16 * NH)
                sp.wait_ge(s_kvst[s], FREE + 16 * (B - 1) * (2 + 4))
            kv_batch(B - 1, 1, False)
            sp.wait_ge(s_mm, C_WO - 4)
            for n in range(2):
                load_qk(0, n, n, n)
                load_v(n, n)
            for s in range(2):
                sp.wait_ge(s_kvst[s], FREE + 16 * B * (2 + 4))

            def attention_loads(kv, b, n, s):
                sp.wait_ge(s_s, QT * n)
                load_qk(kv, b, n + 1, 1 - s)
                sp.wait_ge(s_av, 2 * n)
                load_v(n + 1, 1 - s)

            def loads_of_steps(kv, b0, n_steps):
                with sp.Fori(0, n_steps // 2) as i:
                    for j in range(2):
                        b = b0 + 2 * i + j
                        attention_loads(kv, b + 2, kv * B + b + 1, 1 - j)

            with sp.Fori(0, NKV - 1) as kv:
                loads_of_steps(kv, 0, B - 2)
                for j in range(2):
                    attention_loads(kv + 1, j, kv * B + B - 1 + j, 1 - j)
                with sp.Fori(0, NK // 2) as i:
                    for s in range(2):
                        p = P_WO + 2 + kv * NK + 2 * i + s
                        load_slab(p, s, T_WO + 2 + kv * NK + 2 * i + s)
            loads_of_steps(NKV - 1, 0, B - 2)
            sp.wait_ge(s_t, QT * NKV * B)
            sp.dma_start(BETA, beta.partition_broadcast(P)).then_inc(s_misc, 16)
            sp.dma_start(gate_raw[:, :], gate).then_inc(s_misc, 16)
            for s in range(2):
                sp.dma_start(XIN[s], x[s * P:(s + 1) * P, :]).then_inc(s_xin[s], 16)

            seen = -1
            for g in SEG2:
                if g[0] in ("wo", "fc1", "exp", "fc2") and g[1] != seen:
                    seen = g[1]
                    next_slab(seen)
                if g[0] == "n" and g[2] == 1:
                    r = g[1]
                    sp.wait_ge(s_x2b, r + 1)
                    sp.dma_start(x2_d[r * P:(r + 1) * P, :], XIN[r % 2]).then_inc(s_x2st[r % 2], 16)
                if g[0] == "y" and g[2] == 1 and 1 <= g[1] < RT - 1:
                    r = g[1] - 1
                    sp.wait_ge(s_x2st[r % 2], 16 * (r // 2 + 1))
                    sp.dma_start(XIN[r % 2], x[(r + 2) * P:(r + 3) * P, :]).then_inc(s_xin[r % 2], 16)

            for s in range(2):
                sp.wait_ge(s_x2st[s], 16 * ((RT + 1 - s) // 2))
            sp.wait_ge(s_lo, L_FFN)
            sp.dma_start(GAMMA, gamma.partition_broadcast(P)).then_inc(s_gamma, 16)
            for s in range(2):
                sp.dma_start(XB[s], x2_d[s * P:(s + 1) * P, :]).then_inc(s_xin[s], 16)
            next_slabs(P_FFN, 3 * NK)

            for g in SEG3:
                if g[0] == "down":
                    next_slab(g[1])
                if g[0] == "z" and g[2] == 1:
                    r, s = g[1], g[1] % 2
                    sp.wait_ge(s_o, r + 1)
                    sp.dma_start(out[r * P:(r + 1) * P, :], XB[s]).then_inc(s_out[s], 16)
                    if 1 <= r < RT - 1:
                        sp.wait_ge(s_out[1 - s], 16 * ((r - 1) // 2 + 1))
                        sp.dma_start(XB[1 - s], x2_d[(r + 1) * P:(r + 2) * P, :]).then_inc(s_xin[1 - s], 16)
            for s in range(2):
                sp.wait_ge(s_out[s], 16 * ((RT + 1 - s) // 2))

        @block.gpsimd
        def _(pool):
            pool.memset(ident[:, :], 0.0).then_inc(s_const, 1)
            pool.memset(ones[:, :], 1.0).then_inc(s_const, 1)
            pool.wait_ge(s_const, 2)
            pool.affine_select(out=ident[:, :], in_=ident[:, :], compare_op=ALU.not_equal, fill=1.0, base=0,
                               pattern=[[-1, P]], channel_multiplier=1).then_inc(s_const, 1)

            for n, (free, count) in enumerate([*((q, FREE) for q in (*s_qst, *s_kvst)), (s_avl, 1)]):
                pool.memset(small[:, 212 + n:213 + n], 0.0).then_inc(free, count)

            def slab_lo(p, s):
                pool.wait_ge(s_whi, p + 1)
                pool.tensor_tensor(WS[s][1], RAWS[s], f32(WS[s][0]), ALU.subtract).then_inc(s_wlo, 1)

            def slabs_lo(p0, n):
                with pool.Fori(0, n // 2) as i:
                    for j in range(2):
                        slab_lo(p0 + 2 * i + j, 1 - j)

            def zero_pad(j):
                for l in range(2):
                    pool.memset(f32(HT[j][l][:, :, KEYS:KP]), 0.0).then_inc(s_pad, 1)

            def ctx_lo(b, j):
                pool.wait_ge(s_chi, b + 1)
                pool.tensor_tensor(HT[j][1][:, :, 0:SC], CRAW, f32(HT[j][0][:, :, 0:SC]),
                                   ALU.subtract).then_inc(s_clo, 1)

            slab_lo(0, 0)
            slabs_lo(1, P_Q3 + EDGE)
            slab_lo(P_Q3 + EDGE + 1, 1)
            pool.wait_ge(s_mm, C_Q3 + EDGE)
            pool.wait_ge(s_xt, 16 * 4)
            zero_pad(0)
            ctx_lo(0, 0)
            for p in range(P_Q3 + EDGE + 2, P_WO + 1):
                slab_lo(p, p % 2)
            pool.wait_ge(s_mm, C_KV)
            zero_pad(1)
            ctx_lo(1, 1)
            with pool.Fori(1, B // 2) as i:
                for j in range(2):
                    ctx_lo(2 * i + j, j)
            pool.wait_ge(s_ev, C_SEG1 + len(SEG1))
            pool.memset(YR[:, :], 0.0).then_inc(s_zero, 1)
            pool.wait_ge(s_clo, B)
            pool.memset(FB[:, 0:QT * KP].rearrange("p (i c) -> p i c", i=QT)[:, :, KEYS:KP], 0.0).then_inc(s_zero, 1)

            def p_normalise(n):
                for i in range(QT):
                    pool.wait_ge(s_rec, QT * n + i + 1)
                    pool.tensor_tensor(PR[i], PR[i], rrow[:, i:i + 1].broadcast_to([P, KP]),
                                       ALU.mult).then_inc(s_pn, 1)

            p_normalise(0)
            for s in range(2):
                pool.wait_ge(s_kvst[s], FREE + 16 * B * (2 + 4))
            pool.memset(f32(RD[:, :]), 0.0).then_inc(s_gz, 1)
            with pool.Fori(0, NKV - 1) as kv:
                with pool.Fori(0, B) as i:
                    p_normalise(kv * B + i + 1)
                slabs_lo(P_WO + 1 + kv * NK, NK)
            with pool.Fori(0, B - 1) as i:
                p_normalise((NKV - 1) * B + i + 1)
            pool.wait_ge(s_misc, 32)
            seen = -1
            for g in SEG2:
                if g[0] in ("wo", "fc1", "exp", "fc2") and g[1] != seen:
                    seen = g[1]
                    slab_lo(seen + 1, (seen + 1) % 2)
                if g[0] == "y" and g[2] == 1:
                    r = g[1]
                    pool.wait_ge(s_xn, RT + r + 1)
                    pool.tensor_tensor(XIN[r % 2], XIN[r % 2], BETA, ALU.add).then_inc(s_x2b, 1)
            slabs_lo(P_FFN + 1, N_POS - P_FFN - 2)
            slab_lo(N_POS - 1, 1)

        @block.scalar
        def _(act):
            def slab_hi(p, s, c):
                act.wait_ge(s_raw[s], 8 * p + 16 - 8 * s)
                act.wait_ge(s_mm, c)
                act.activation(WS[s][0], RAWS[s], ACT.Copy).then_inc(s_whi, 1)

            def next_hi(p0, n, c0):
                with act.Fori(0, n // 2) as i:
                    for s in range(2):
                        slab_hi(p0 + 1 + 2 * i + s, 1 - s, c0 + 4 * i + 2 * s)

            def hi(c, dst, src, scale=1.0):
                act.wait_ge(s_mm, c + 1)
                act.activation(dst, src, ACT.Copy, scale=scale).then_inc(s_hi, 1)

            def sqrt_var(r, n):
                act.wait_ge(s_agg, n + 1)
                act.activation(sd[:, r:r + 1], mv[:, r, 1:2], ACT.Sqrt, bias=eps_ap).then_inc(s_sd, 1)

            def rows_hi(xt, r, h, c):
                hi(c, row_tile(xt, 0, r, h), gb(c)[:, :].rearrange("p (k n) -> p k n", k=4))

            def q_hi(c, c_static, h, slot, freed):
                act.wait_ge(s_qst[slot], FREE + freed)
                n = PARTS[h][1] - PARTS[h][0]
                hi(c, QSTV[slot][:, 0, 0:n], gb(c_static)[:, 0:n], SCALE)

            def split_piece(j):
                act.wait_ge(s_piece[j % 3], 16 * (j // 3 + 1))
                act.activation(WKV[j][0], PRAW[j], ACT.Copy).then_inc(s_phi, 1)

            eps_ap = small[:, 208:209]
            act.wait_ge(s_link, 1)
            seen = -1
            for r in range(2):
                sqrt_var(r, r)
            for j, g in enumerate(SEG1):
                c = C_SEG1 + j
                if g[0] == "ln":
                    _, r, h = g
                    if h == 0 and r + 2 < RT:
                        sqrt_var(r + 2, r + 2)
                    rows_hi(XT, r, h, c)
                    if r == 2 and h == 1:
                        slab_hi(0, 0, c)
                else:
                    _, p, m, h = g
                    slab_hi(p + 1, (p + 1) % 2, c)
                    q_hi(c, c, h, p % 2, 16 * (p // 2))
                    if h == 1:
                        split_piece(2 * m)
                        split_piece(2 * m + 1)
                    if p == EDGE - 1:
                        act.wait_ge(s_ev, c)
                        for h_, (first, end) in enumerate(PARTS):
                            for l in range(2):
                                act.dma_start(xt_d[:, l, :, first:end], f32(XT[h_][l])).then_inc(s_xt, 16)

            with act.Fori(0, (NH - 2 * EDGE) // 2) as i:
                for s in range(2):
                    c = C_Q2 + 4 * i + 2 * s
                    slab_hi(P_Q2 + 2 * i + s + 1, 1 - s, c)
                    for h in range(2):
                        q_hi(c + h, C_Q2 + 2 * s + h, h, h, 16 * EDGE + 32 * i + 16 * s)

            def ctx_hi(b, j, c):
                act.wait_ge(s_ctx, 16 * (b + 1))
                act.wait_ge(s_mm, c)
                act.activation(HT[j][0][:, :, 0:SC], CRAW, ACT.Copy).then_inc(s_chi, 1)

            for j, g in enumerate(SEG_Q3):
                _, p, m, h = g
                c = C_Q3 + j
                slab_hi(p + 1, (p + 1) % 2, c)
                if j == EDGE:
                    act.wait_ge(s_xt, 16 * 4)
                    ctx_hi(0, 0, c)
                q_hi(c, c, h, p % 2, 16 * (NH - EDGE + (j // 2)))

            def kv_hi(b, j, before, more):
                if more:
                    ctx_hi(b + 1, 1 - j, C_KV + 8 * b)
                for u in range(8):
                    s, c = u % 2, C_KV + u
                    p, n = (P, KP) if u < 4 else (KT, 512)
                    act.wait_ge(s_kvst[s], FREE + before + [0, 0, 16, 16, 32, 32, 64, 64][u])
                    hi(C_KV + 8 * b + u, KVST[s][0][0:p, 0:n], gb(c)[0:p, 0:n])

            for s in range(2):
                act.wait_ge(s_qst[s], FREE + 16 * NH)
            with act.Fori(0, B // 2 - 1) as i:
                for j in range(2):
                    kv_hi(2 * i + j, j, (2 * i + j) * 96, True)
            kv_hi(B - 2, 0, (B - 2) * 96, True)
            kv_hi(B - 1, 1, (B - 1) * 96, False)

            def exp(n, i):
                act.wait_ge(s_max, QT * n + i + 1)
                act.activation(PR[i][:, 0:KEYS], SB[i % 3][:, 0:KEYS], ACT.Exp, bias=negmax[:, i:i + 1],
                               accum_out=rowsum[:, i:i + 1]).then_inc(s_exp, 1)

            def attention(n, b, scores, av):
                for i in range(QT):
                    if av:
                        act.wait_ge(s_t, QT * (n - 1) + i + 1)
                        act.activation(PT[0][0:KT, :, i * P:(i + 1) * P],
                                       TB[i % 3][0:KT, :].rearrange("p (t n) -> p t n", t=4),
                                       ACT.Copy).then_inc(s_pth, 1)
                    if scores and i >= 2:
                        exp(n, i - 2)
                if scores:
                    exp(n, QT - 2)
                    exp(n, QT - 1)
                if av:
                    for a in range(2):
                        act.wait_ge(s_av, 2 * (n - 1) + a + 1)
                        act.activation(AT[0][:, 4 * a:4 * a + 4, bass.ds(b * SQ, SQ)],
                                       AV[a][:, 0:QH].rearrange("p (g n) -> p g n", g=4), ACT.Copy).then_inc(s_avh, 1)

            act.wait_ge(s_zero, 2)
            attention(0, 0, True, False)
            with act.Fori(0, NKV - 1) as kv:
                with act.Fori(0, B) as b:
                    attention(kv * B + b + 1, b, True, True)
                next_hi(P_WO + kv * NK, NK, C_WO + kv * 2 * NK)
            with act.Fori(0, B - 1) as b:
                attention((NKV - 1) * B + b + 1, b, True, True)
            attention(NKV * B, B - 1, False, True)

            act.wait_ge(s_misc, 32)
            act.wait_ge(s_gz, 1)
            act.activation(GT[0][:, :, 0:NE], gate_raw[:, :].rearrange("p (k e) -> p k e", k=NK),
                           ACT.Copy).then_inc(s_phi, 1)
            seen = -1
            for j, g in enumerate(SEG2):
                c, what = C_SEG2 + j, g[0]
                if what in ("wo", "fc1", "exp", "fc2") and g[1] != seen:
                    seen = g[1]
                    slab_hi(seen + 1, (seen + 1) % 2, c)
                if what == "y" and g[2] == 1:
                    sqrt_var(g[1], RT + g[1])
                if what == "n":
                    rows_hi(X2, g[1], g[2], c)
                if what == "fc1":
                    n = PARTS[g[3]][1] - PARTS[g[3]][0]
                    hi(c, IN[g[3]][0][:, g[2], :], gb(c)[:, 0:n])
                if what == "exp":
                    n = PARTS[g[3]][1] - PARTS[g[3]][0]
                    act.wait_ge(s_ev, c + 1)
                    act.activation(IN[g[3]][0][:, 4 + g[2], :], SQT[:, 0:n], ACT.Copy).then_inc(s_hi, 1)

            def up(p0, c0):
                with act.Fori(0, NK // 2) as i:
                    for s in range(2):
                        m = 2 * i + s
                        slab_hi(p0 + 1 + m, 1 - s, c0 + 2 * m)
                        for h, (first, end) in enumerate(PARTS):
                            c, n = c0 + 2 * m + h, end - first
                            act.wait_ge(s_mm, c + 1)
                            act.activation(RELU[:, 0:n], gb(C_FFN + 2 * s + h)[:, 0:n], ACT.Relu).then_inc(s_relu, 1)
                            act.wait_ge(s_ev, c + 1)
                            act.activation(IN[h][0][:, m, :], SQT[:, 0:n], ACT.Copy).then_inc(s_hi, 1)

            up(P_FFN, C_FFN)
            next_hi(P_FFN + NK, NK, C_FFN + 2 * NK)
            up(P_FFN + 2 * NK, C_FFN + 4 * NK)

            for j, g in enumerate(SEG3):
                if g[0] == "down" and g[1] + 1 < N_POS:
                    slab_hi(g[1] + 1, (g[1] + 1) % 2, C_SEG3 + j)
                if g[0] == "z" and g[2] == 1:
                    sqrt_var(g[1], 2 * RT + g[1])

        @block.vector
        def _(dve):
            chain = [0]

            def link(ins):
                chain[0] += 1
                ins.then_inc(s_link, 1)
                dve.wait_ge(s_link, chain[0])

            def lo(c, h, dst, src, hi_of):
                dve.wait_ge(s_hi, h + 1)
                dve.tensor_tensor(dst, src, f32(hi_of), ALU.subtract).then_inc(s_ev, 1)

            def rows_lo(xt, r, h, c, nh):
                lo(c, nh, row_tile(xt, 1, r, h), gb(c)[:, :].rearrange("p (k n) -> p k n", k=4), row_tile(xt, 0, r, h))

            def mean_var(r, n, halves):
                for h in range(2):
                    ins = dve.bn_stats(stats[:, 6 * h:6 * h + 6], halves[h])
                link(ins)
                dve.bn_aggr(mv[:, r, :], stats).then_inc(s_agg, 1)
                dve.wait_ge(s_agg, n + 1)

            def reciprocal_sd(r, n):
                dve.wait_ge(s_sd, n + 1)
                link(dve.reciprocal(rs[:, r:r + 1], sd[:, r:r + 1]))

            def normalise(r, n, dst, src):
                reciprocal_sd(r, n)
                dve.tensor_scalar(dst, src, mv[:, r, 0:1], rs[:, r:r + 1], ALU.subtract, ALU.mult).then_inc(s_xn, 1)

            link(dve.memset(small[:, 208:209], EPS))

            def piece_lo(j):
                dve.wait_ge(s_phi, j + 1)
                dve.tensor_tensor(WKV[j][1], PRAW[j], f32(WKV[j][0]), ALU.subtract).then_inc(s_plo, 1)

            def q_lo(nh, c_static, h, slot):
                n = PARTS[h][1] - PARTS[h][0]
                dve.wait_ge(s_hi, nh + 1)
                dve.scalar_tensor_tensor(out=QSTV[slot][:, 1, 0:n], in0=gb(c_static)[:, 0:n], scalar=SCALE,
                                         in1=f32(QSTV[slot][:, 0, 0:n]), op0=ALU.mult, op1=ALU.subtract).then_inc(s_ev, 1)

            def x_stats(r):
                dve.wait_ge(s_x[r], 16)
                mean_var(r, r, [X7[:, r, 0:512], X7[:, r, 512:1024]])

            for r in range(2):
                x_stats(r)
            normalise(0, 0, X7[:, 0, :], X7[:, 0, :])
            for j, g in enumerate(SEG1):
                c = C_SEG1 + j
                if g[0] == "ln":
                    _, r, h = g
                    if h == 0:
                        if r + 2 < RT:
                            x_stats(r + 2)
                        if r + 1 < RT:
                            normalise(r + 1, r + 1, X7[:, r + 1, :], X7[:, r + 1, :])
                    rows_lo(XT, r, h, c, H_SEG1[j])
                else:
                    _, p, m, h = g
                    q_lo(H_SEG1[j], c, h, p % 2)
                    if h == 1:
                        piece_lo(2 * m)
                        piece_lo(2 * m + 1)

            with dve.Fori(0, (NH - 2 * EDGE) // 2) as i:
                for s in range(2):
                    for h in range(2):
                        q_lo(H_Q2 + 4 * i + 2 * s + h, C_Q2 + 2 * s + h, h, h)
            for j, g in enumerate(SEG_Q3):
                q_lo(H_Q3[j], C_Q3 + j, g[3], g[1] % 2)

            with dve.Fori(0, B) as b:
                for u in range(8):
                    s = u % 2
                    p, n = (P, KP) if u < 4 else (KT, 512)
                    lo(None, H_KV + 8 * b + u, KVST[s][1][0:p, 0:n], gb(C_KV + u)[0:p, 0:n], KVST[s][0][0:p, 0:n])

            def reciprocal_sum(n, i):
                dve.wait_ge(s_exp, QT * n + i + 1)
                dve.reciprocal(rrow[:, i:i + 1], rowsum[:, i:i + 1]).then_inc(s_rec, 1)

            def max_of(n, i):
                dve.wait_ge(s_s, QT * n + i + 1)
                dve.reduce_max(negmax[:, i:i + 1], SB[i % 3][:, 0:KEYS], AX.X, negate=True).then_inc(s_max, 1)

            def attention(n, b, scores, av):
                for i in range(QT):
                    if av:
                        dve.wait_ge(s_pth, QT * (n - 1) + i + 1)
                        cols = slice(i * P, (i + 1) * P)
                        dve.tensor_tensor(PT[1][0:KT, :, cols], TB[i % 3][0:KT, :].rearrange("p (t n) -> p t n", t=4),
                                          f32(PT[0][0:KT, :, cols]), ALU.subtract).then_inc(s_ptl, 1)
                    if scores:
                        if i >= 1:
                            max_of(n, i - 1)
                        if i >= 3:
                            reciprocal_sum(n, i - 3)
                if scores:
                    max_of(n, QT - 1)
                    for i in range(QT - 3, QT):
                        reciprocal_sum(n, i)
                if av:
                    for a in range(2):
                        dve.wait_ge(s_avh, 2 * (n - 1) + a + 1)
                        at_ = (slice(None), slice(4 * a, 4 * a + 4), bass.ds(b * SQ, SQ))
                        dve.tensor_tensor(AT[1][at_], AV[a][:, 0:QH].rearrange("p (g n) -> p g n", g=4),
                                          f32(AT[0][at_]), ALU.subtract).then_inc(s_avl, 1)

            def add_to_y(c, c_static, m, h):
                dve.wait_ge(s_mm, c + 1)
                cols = slice(*PARTS[h])
                dve.tensor_tensor(Y[:, m, cols], Y[:, m, cols], gb(c_static)[:, 0:PARTS[h][1] - PARTS[h][0]],
                                  ALU.add).then_inc(s_ev, 1)

            def y_slabs(c0, c_static):
                with dve.Fori(0, NK // 2) as i:
                    for s in range(2):
                        for h in range(2):
                            add_to_y(c0 + 4 * i + 2 * s + h, c_static + 2 * s + h, 2 * i + s, h)

            dve.wait_ge(s_zero, 2)
            attention(0, 0, True, False)
            with dve.Fori(0, NKV - 1) as kv:
                with dve.Fori(0, B) as b:
                    attention(kv * B + b + 1, b, True, True)
                y_slabs(C_WO + kv * 2 * NK, C_WO)
            with dve.Fori(0, B - 1) as b:
                attention((NKV - 1) * B + b + 1, b, True, True)
            attention(NKV * B, B - 1, False, True)

            dve.wait_ge(s_phi, 9)
            dve.tensor_tensor(GT[1][:, :, 0:NE], gate_raw[:, :].rearrange("p (k e) -> p k e", k=NK),
                              f32(GT[0][:, :, 0:NE]), ALU.subtract).then_inc(s_gs, 1)

            def x2_tile(c, r, h):
                cols = slice(512 * h, 512 * h + 512)
                dve.wait_ge(s_mm, c + 1)
                if h == 0:
                    dve.wait_ge(s_xin[r % 2], 16 * (r // 2 + 1))
                dve.tensor_tensor(XIN[r % 2][:, cols], XIN[r % 2][:, cols], gb(c)[:, :], ALU.add).then_inc(s_ev, 1)
                if h == 1:
                    dve.wait_ge(s_ev, c + 1)
                    mean_var(r, RT + r, [XIN[r % 2][:, 0:512], XIN[r % 2][:, 512:1024]])
                    normalise(r, RT + r, XN, XIN[r % 2])

            def routing_weights(c):
                dve.tensor_copy(lg, gb(c)[:, 0:RT * NE]).then_inc(s_ev, 1)
                dve.wait_ge(s_ev, c + 1)
                for r in range(RT):
                    ins = dve.max(top8[:, r * NE:(r + 1) * NE], lg[:, r * NE:(r + 1) * NE])
                link(ins)
                best = top8.rearrange("p (r e) -> p r e", e=NE)
                link(dve.tensor_tensor(rw.rearrange("p (r e) -> p r e", e=1), best[:, :, 0:1], best[:, :, 1:2], ALU.add))
                for s in range(2):
                    dve.wait_ge(s_x2st[s], 16 * ((RT + 1 - s) // 2))
                for r in range(RT):
                    dve.tensor_scalar(RWREP[:, r, :], ones[:, :], rw[:, r:r + 1], None, ALU.mult).then_inc(s_rw, 1)

            n_lo = 0
            for j, g in enumerate(SEG2):
                c, what = C_SEG2 + j, g[0]
                if len(g) == 4:
                    h, n, cols = g[3], PARTS[g[3]][1] - PARTS[g[3]][0], slice(*PARTS[g[3]])
                if what == "wo":
                    add_to_y(c, c, g[2], h)
                elif what == "y":
                    x2_tile(c, g[1], g[2])
                elif what == "n":
                    rows_lo(X2, g[1], g[2], c, H_SEG2[j])
                elif what == "fc1":
                    lo(c, H_SEG2[j], IN[h][1][:, g[2], :], gb(c)[:, 0:n], IN[h][0][:, g[2], :])
                elif what == "logit":
                    dve.wait_ge(s_mm, c + 1)
                    dve.tensor_copy(LGT[0:NE, cols], gb(c)[0:NE, 0:n]).then_inc(s_ev, 1)
                elif what == "logitT":
                    dve.wait_ge(s_mm, c + 1)
                    routing_weights(c)
                elif what == "routing":
                    cols = slice(*PARTS[g[1]])
                    dve.wait_ge(s_mm, c + 1)
                    dve.tensor_copy(RWB[:, cols], gb(c)[:, 0:cols.stop - cols.start]).then_inc(s_ev, 1)
                elif what == "exp":
                    dve.wait_ge(s_mm, c + 1)
                    dve.wait_ge(s_ev, c)
                    if n_lo:
                        dve.wait_ge(s_lo, n_lo)
                    dve.tensor_tensor(SQT[:, 0:n], gb(c)[:, 0:n], RWB[:, cols], ALU.mult).then_inc(s_ev, 1)
                    dve.wait_ge(s_hi, H_SEG2[j] + 1)
                    dve.tensor_tensor(IN[h][1][:, 4 + g[2], :], SQT[:, 0:n], f32(IN[h][0][:, 4 + g[2], :]),
                                      ALU.subtract).then_inc(s_lo, 1)
                    n_lo += 1
                elif what == "fc2":
                    dve.wait_ge(s_mm, c + 1)
                    dve.tensor_copy(Y[:, g[2], cols], gb(c)[:, 0:n]).then_inc(s_ev, 1)

            def up(f):
                with dve.Fori(0, NK // 2) as i:
                    for s in range(2):
                        for h, (first, end) in enumerate(PARTS):
                            n, w = f * 2 * NK + 4 * i + 2 * s + h, end - first
                            dve.wait_ge(s_lo, L_FFN + n)
                            dve.wait_ge(s_relu, n + 1)
                            dve.scalar_tensor_tensor(out=SQT[:, 0:w], in0=gb(C_FFN + 2 * s + h)[:, 0:w], scalar=0.0,
                                                     in1=RELU[:, 0:w], op0=ALU.max, op1=ALU.mult).then_inc(s_ev, 1)
                            dve.wait_ge(s_hi, H_FFN + n + 1)
                            dve.tensor_tensor(IN[h][1][:, 2 * i + s, :], SQT[:, 0:w], f32(IN[h][0][:, 2 * i + s, :]),
                                              ALU.subtract).then_inc(s_lo, 1)

            up(0)
            y_slabs(C_FFN + 2 * NK, C_FFN)
            up(1)

            dve.wait_ge(s_gamma, 16)

            def last_layernorm(c, r):
                s = r % 2
                dve.wait_ge(s_mm, c + 2)
                mean_var(r, 2 * RT + r, [gb(c)[:, :], gb(c + 1)[:, :]])
                reciprocal_sd(r, 2 * RT + r)
                if r >= 1:
                    dve.wait_ge(s_o, r)
                for h in range(2):
                    cols = slice(512 * h, 512 * h + 512)
                    dve.scalar_tensor_tensor(out=CEN[:, cols], in0=gb(c + h)[:, :], scalar=mv[:, r, 0:1],
                                             in1=GAMMA[:, cols], op0=ALU.subtract, op1=ALU.mult).then_inc(s_ev, 1)
                dve.wait_ge(s_ev, c + 2)
                dve.wait_ge(s_xin[s], 16 * ((RT + 1 - s) // 2 + r // 2 + 1))
                dve.scalar_tensor_tensor(out=XB[s], in0=CEN, scalar=rs[:, r:r + 1], in1=XB[s],
                                         op0=ALU.mult, op1=ALU.add).then_inc(s_o, 1)

            for j, g in enumerate(SEG3):
                c = C_SEG3 + j
                if g[0] == "down":
                    add_to_y(c, c, g[2], g[3])
                elif g[2] == 0:
                    last_layernorm(c, g[1])

        @block.tensor
        def _(pe):
            def bank_free(c):
                pe.wait_ge(s_ev, c - 3)

            def three(out_ap, w, a, first, last):
                pe.matmul(out_ap, w[0], a[0], start=first, stop=False)
                pe.matmul(out_ap, w[0], a[1], start=False, stop=False)
                return pe.matmul(out_ap, w[1], a[0], start=False, stop=last)

            def product(s, acts, h, k0, nk, w0, c, c_static):
                bank_free(c)
                n = PARTS[h][1] - PARTS[h][0]
                for k in range(nk):
                    w = [WS[s][l][:, (w0 + k) * P:(w0 + k + 1) * P] for l in range(2)]
                    last = three(gb(c_static)[:, 0:n], w, [acts(l, k0 + k, h) for l in range(2)], k == 0, k == nk - 1)
                last.then_inc(s_mm, 1)

            def of_parts(tiles):
                return lambda l, k, h: tiles[h][l][:, k, :]

            def of_attention(l, k, h):
                return AT[l][:, k, PARTS[h][0]:PARTS[h][1]]

            seen = [-1]

            def slab_split(p):
                if seen[0] != p:
                    seen[0] = p
                    pe.wait_ge(s_wlo, p + 1)

            def transposes(c, src):
                if c >= 4:
                    bank_free(c)
                for k in range(4):
                    last = pe.transpose(gb(c)[:, k * P:(k + 1) * P], src(k), ident[:, :])
                last.then_inc(s_mm, 1)

            pe.wait_ge(s_const, 3)
            for j, g in enumerate(SEG1):
                c = C_SEG1 + j
                if g[0] == "ln":
                    _, r, h = g
                    if h == 0:
                        pe.wait_ge(s_xn, r + 1)
                    transposes(c, lambda k: X7[:, r, (4 * h + k) * P:(4 * h + k + 1) * P])
                else:
                    _, p, m, h = g
                    if m == 0:
                        pe.wait_ge(s_ev, 8 if h == 0 else c)
                    slab_split(p)
                    product(p % 2, of_parts(XT), h, 0, NK, 0, c, c)

            with pe.Fori(0, (NH - 2 * EDGE) // 2) as i:
                for s in range(2):
                    pe.wait_ge(s_wlo, P_Q2 + 2 * i + s + 1)
                    for h in range(2):
                        product(s, of_parts(XT), h, 0, NK, 0, C_Q2 + 4 * i + 2 * s + h, C_Q2 + 2 * s + h)
            for j, (_, p, m, h) in enumerate(SEG_Q3):
                slab_split(p)
                product(p % 2, of_parts(XT), h, 0, NK, 0, C_Q3 + j, C_Q3 + j)

            pe.wait_ge(s_plo, 8)

            def wkv(which, k, l, first, n):
                return WKV[which * 4 + k // 2][l][:, (k % 2) * 512 + first:(k % 2) * 512 + first + n]

            with pe.Fori(0, B // 2) as i:
                for j in range(2):
                    b = 2 * i + j
                    pe.wait_ge(s_pad, 2 * j + 2)
                    pe.wait_ge(s_clo, b + 1)
                    pe.wait_ge(s_lat[j], 32 * (i + 1))
                    for u in range(8):
                        bank_free(C_KV + 8 * b + u)
                        dst = gb(C_KV + u)
                        for k in range(NK):
                            if u < 4:
                                last = three(dst[:, 0:KP], [wkv(0, k, l, u * D, D) for l in range(2)],
                                             [HT[j][l][:, k, :] for l in range(2)], k == 0, k == NK - 1)
                            else:
                                last = three(dst[0:KT, :], [HT[j][l][:, k, (u - 4) * KT:(u - 3) * KT] for l in range(2)],
                                             [wkv(1, k, l, 0, 512) for l in range(2)], k == 0, k == NK - 1)
                        last.then_inc(s_mm, 1)

            def av(s, a, ts):
                for t in ts:
                    last = three(AV[a][:, 0:QH],
                                 [VB[s][0:KT, (l * 4 + t) * D:(l * 4 + t + 1) * D] for l in range(2)],
                                 [PT[l][0:KT, t, a * QH:(a + 1) * QH] for l in range(2)], t == 0, t == 3)
                return last

            def attention(n, s, loads, scores, with_av, ev):
                for i in range(QT):
                    if with_av:
                        pe.wait_ge(s_pn, QT * (n - 1) + i + 1)
                        if i < 3 and ev is not None:
                            pe.wait_ge(s_ev, ev - 3 + LAST_USE[i])
                        if i >= 3:
                            pe.wait_ge(s_ptl, QT * (n - 1) + i - 2)
                        for t in range(4):
                            last = pe.transpose(TB[i % 3][0:KT, t * P:(t + 1) * P], PR[i][:, t * KT:(t + 1) * KT],
                                                ident[:, :])
                        last.then_inc(s_t, 1)
                    if scores:
                        if i == 0:
                            pe.wait_ge(s_qk[s], loads)
                        if i >= 3 or with_av:
                            pe.wait_ge(s_exp, QT * n + max(i - 2, 0))
                        three(SB[i % 3][:, 0:KP], [QB[s][:, l * QC + i * P:l * QC + (i + 1) * P] for l in range(2)],
                              [KB[s][:, l * KP:(l + 1) * KP] for l in range(2)], True, True).then_inc(s_s, 1)
                    if with_av:
                        if i == 5:
                            pe.wait_ge(s_v[1 - s], loads_of_v(n, s))
                            pe.wait_ge(s_ptl, QT * (n - 1) + 4)
                            pe.wait_ge(s_avl, 1 + 2 * (n - 1))
                            if ev is not None:
                                pe.wait_ge(s_ev, ev - 3 + LAST_USE[3])
                            av(1 - s, 0, [0, 1])
                        if i == 6:
                            av(1 - s, 0, [2, 3]).then_inc(s_av, 1)
                            pe.wait_ge(s_ptl, QT * n)
                            av(1 - s, 1, range(4)).then_inc(s_av, 1)

            def loads_of_v(n, s):
                return 8 * (n + 1) if s == 1 else 8 * n

            def loads_of_qk(n, s):
                return 24 * (n + 1) if s == 1 else 24 * (n + 2)

            attention(0, 0, 48, True, False, None)
            with pe.Fori(0, NKV - 1) as kv:
                with pe.Fori(0, B // 2) as i:
                    for j in range(2):
                        n = kv * B + 2 * i + j + 1
                        attention(n, 1 - j, loads_of_qk(n, 1 - j), True, True,
                                  C_WO + kv * 2 * NK if j == 0 else None)
                with pe.Fori(0, NK // 2) as i:
                    for s in range(2):
                        m = 2 * i + s
                        pe.wait_ge(s_wlo, P_WO + kv * NK + m + 1)
                        for h in range(2):
                            pe.wait_ge(s_avl, 1 + 2 * B * kv + (10, 2 * B)[h])
                            product(s, of_attention, h, 0, G, 0, C_WO + kv * 2 * NK + 2 * m + h, C_WO + 2 * s + h)
            with pe.Fori(0, B // 2 - 1) as i:
                for j in range(2):
                    n = (NKV - 1) * B + 2 * i + j + 1
                    attention(n, 1 - j, loads_of_qk(n, 1 - j), True, True, C_SEG2 if j == 0 else None)
            n = NKV * B - 1
            attention(n, 1, loads_of_qk(n, 1), True, True, None)
            attention(n + 1, 0, 0, False, True, None)

            ev_of = {}
            for j, g in enumerate(SEG2):
                c, what = C_SEG2 + j, g[0]
                if what in ("wo", "fc1", "exp", "fc2"):
                    slab_split(g[1])
                if what == "wo":
                    pe.wait_ge(s_avl, 1 + 2 * B * (NKV - 1) + (10 if j == 0 else 2 * B))
                    product(g[1] % 2, of_attention, g[3], 0, G, 0, c, c)
                elif what == "y":
                    if g[2] == 0:
                        pe.wait_ge(s_ev, ev_of["wo", int(g[1] >= 4)])
                    transposes(c, lambda k: Y[:, 4 * g[2] + k, g[1] * P:(g[1] + 1) * P])
                elif what == "n":
                    if g[2] == 0:
                        pe.wait_ge(s_xn, RT + g[1] + 1)
                    transposes(c, lambda k: XN[:, (4 * g[2] + k) * P:(4 * g[2] + k + 1) * P])
                elif what == "fc1":
                    pe.wait_ge(s_ev, ev_of["n", g[3]])
                    product(g[1] % 2, of_parts(X2), g[3], 0, NK, 0, c, c)
                elif what == "logit":
                    pe.wait_ge(s_gs, 1)
                    pe.wait_ge(s_ev, ev_of["n", g[3]])
                    bank_free(c)
                    for k in range(NK):
                        last = three(gb(c)[:, 0:PARTS[g[3]][1] - PARTS[g[3]][0]], [GT[l][:, k, :] for l in range(2)],
                                     [X2[g[3]][l][:, k, :] for l in range(2)], k == 0, k == NK - 1)
                    last.then_inc(s_mm, 1)
                elif what == "logitT":
                    bank_free(c)
                    pe.wait_ge(s_ev, ev_of["logit", 1])
                    for r in range(RT):
                        last = pe.transpose(gb(c)[:, r * NE:(r + 1) * NE], LGT[0:NE, r * P:(r + 1) * P],
                                            ident[0:NE, 0:NE])
                    last.then_inc(s_mm, 1)
                elif what == "routing":
                    bank_free(c)
                    tiles = (range(0, 4), range(4, RT))[g[1]]
                    pe.wait_ge(s_rw, tiles[-1] + 1)
                    for r in tiles:
                        last = pe.transpose(gb(c)[:, (r % 4) * P:(r % 4 + 1) * P], RWREP[:, r, :], ident[:, :])
                    last.then_inc(s_mm, 1)
                elif what == "exp":
                    pe.wait_ge(s_ev, ev_of["fc1", g[3]])
                    product(g[1] % 2, of_parts(IN), g[3], 0, 4, 4 * (g[2] % 2), c, c)
                elif what == "fc2":
                    pe.wait_ge(s_lo, L_FFN - 1 + g[3])
                    product(g[1] % 2, of_parts(IN), g[3], 4, 4, 4 * (g[2] % 2), c, c)
                if len(g) == 4:
                    ev_of[what, g[3]] = c + 1
                if what == "n":
                    ev_of[what, g[1] // 4] = c + 1

            def layer(p0, c0, tiles, ready):
                with pe.Fori(0, NK // 2) as i:
                    for s in range(2):
                        m = 2 * i + s
                        pe.wait_ge(s_wlo, p0 + m + 1)
                        for h in range(2):
                            if ready is not None:
                                pe.wait_ge(s_lo, ready - 1 + h)
                            product(s, of_parts(tiles), h, 0, NK, 0, c0 + 2 * m + h, C_FFN + 2 * s + h)

            layer(P_FFN, C_FFN, X2, None)
            layer(P_FFN + NK, C_FFN + 2 * NK, IN, L_FFN + 2 * NK)
            layer(P_FFN + 2 * NK, C_FFN + 4 * NK, X2, None)

            for j, g in enumerate(SEG3):
                c = C_SEG3 + j
                if g[0] == "down":
                    slab_split(g[1])
                    pe.wait_ge(s_lo, L_FFN + 4 * NK - 1 + g[3])
                    product(g[1] % 2, of_parts(IN), g[3], 0, NK, 0, c, c)
                    ev_of["down", g[3]] = c + 1
                else:
                    if g[2] == 0:
                        pe.wait_ge(s_ev, ev_of["down", int(g[1] >= 4)])
                    transposes(c, lambda k: Y[:, 4 * g[2] + k, g[1] * P:(g[1] + 1) * P])


def kernel(x, ctx_4096, L0_xattn_Wq, L0_xattn_Wk, L0_xattn_Wv, L0_xattn_Wo, L0_ffn_gate_w, L0_ffn_up_w,
           L0_ffn_down_w, L0_ffn_fc1_w, L0_ffn_fc2_w, L0_ffn_expert_w, L0_ffn_ln_gamma, L0_ffn_ln_beta):
    import numpy as np
    import concourse.bacc as bacc
    from concourse import mybir as mb
    from concourse.bass_utils import run_bass_kernel_spmd

    def tiles(w, nk, per):
        w = np.asarray(w)
        k, m = w.shape
        a = w.reshape(k // (nk * P), nk, P, m // (per * P), per, P)
        return a.transpose(0, 3, 2, 4, 1, 5).reshape(-1, P, per * nk * P)

    up, down = np.asarray(L0_ffn_up_w), np.asarray(L0_ffn_down_w)
    slabs = np.concatenate([
        tiles(L0_xattn_Wq, NK, 1), tiles(L0_xattn_Wo, G, 1), tiles(L0_ffn_fc1_w, NK, 1),
        tiles(L0_ffn_expert_w, 4, 2), tiles(L0_ffn_fc2_w, 4, 2),
        tiles(up[:, 0:1024], NK, 1), tiles(down[0:1024], NK, 1),
        tiles(up[:, 1024:2048], NK, 1), tiles(down[1024:2048], NK, 1)])
    wkv = np.concatenate([np.asarray(w).reshape(4, 2, P, 512).transpose(0, 2, 1, 3).reshape(4, P, 1024)
                          for w in (L0_xattn_Wk, L0_xattn_Wv)])
    ctxT = np.asarray(ctx_4096).reshape(B, SC, NK, P).transpose(0, 3, 2, 1)
    gate = np.asarray(L0_ffn_gate_w).reshape(NK, P, NE).transpose(1, 0, 2).reshape(P, NK * NE)
    laid = {"x": np.asarray(x).reshape(ROWS, HID), "ctxT": ctxT, "slabs": slabs, "wkv": wkv, "gate": gate,
            "gamma": L0_ffn_ln_gamma, "beta": L0_ffn_ln_beta}

    nc = bacc.Bacc("TRN2", target_bir_lowering=False, num_devices=1)
    arrays, args = {}, []
    for name, a in laid.items():
        a = np.ascontiguousarray(a)
        arrays[f"in_{name}"] = a
        args.append(nc.dram_tensor(f"in_{name}", a.shape, mb.dt.from_np(a.dtype), kind="ExternalInput").ap())
    args.append(nc.dram_tensor("out", (ROWS, HID), mb.dt.float32, kind="ExternalOutput").ap())
    xattn_ffn(nc, *args)
    r = run_bass_kernel_spmd(nc, [arrays], core_ids=[0])
    return r.results[0]["out"].reshape(B, SQ, HID)
```

```python
from contextlib import ExitStack

import concourse.bass as bass
from concourse import mybir

F32 = mybir.dt.float32
F32R = mybir.dt.float32r
ALU = mybir.AluOpType
ACT = mybir.ActivationFunctionType
AX = mybir.AxisListType

P = 128
B, SQ, HID = 8, 112, 1024
SC = 375
NH, NKV, D = 32, 4, 128
G = NH // NKV
INT, LAT, NE = 2048, 512, 8
KEYS = SC + SQ
KP = 488
KT = KP // 4
ROWS = B * SQ
RT = ROWS // P
PARTS = ((0, 4 * P), (4 * P, ROWS))
NK = HID // P
QC = G * SQ
QT = QC // P
QH = QC // 2
SLAB = NK * P
SCALE = float(D) ** -0.5
XT_STORED = 16 * NK * 4
FREE = 16
EPS = 1e-5

T_Q = 0
T_WO = T_Q + NH
T_FC1 = T_WO + NKV * NK
T_EXP = T_FC1 + LAT // P
T_FC2 = T_EXP + LAT // P // 2
T_FFN = T_FC2 + HID // P // 2
N_SLABS = T_FFN + 4 * NK

EDGE = 4
SLAB_AT = (2 * list(range(EDGE)) + list(range(EDGE, NH - EDGE)) + 2 * list(range(NH - EDGE, NH))
           + list(range(T_WO, T_FC1)) + list(range(T_FC1 - NK, T_FC1))
           + 2 * list(range(T_FC1, T_EXP)) + list(range(T_EXP, N_SLABS)) + list(range(N_SLABS - NK, N_SLABS)))
P_Q2 = 2 * EDGE
P_Q3 = P_Q2 + NH - 2 * EDGE
P_WO = P_Q3 + 2 * EDGE
P_SEG2 = P_WO + (NKV - 1) * NK
P_FC1 = P_SEG2 + 2 * NK
P_EXP = P_FC1 + 2 * (LAT // P)
P_FC2 = P_EXP + LAT // P // 2
P_FFN = P_FC2 + HID // P // 2
P_SEG3 = P_FFN + 3 * NK
N_POS = P_SEG3 + 2 * NK
assert N_POS == len(SLAB_AT)


def both(what, r):
    return [(what, r, 0), (what, r, 1)]


def weave(products, between):
    return [g for j, p in enumerate(products) for g in [p] + between.get(j, [])]


SEG1 = [g for r in range(4) for g in both("ln", r)] + weave(
    [("q", h * EDGE + m, m, h) for h in range(2) for m in range(EDGE)], {j: both("ln", 4 + j) for j in range(3)})
SEG_Q3 = [("q", P_Q3 + h * EDGE + m, NH - EDGE + m, h) for h in range(2) for m in range(EDGE)]
SEG2 = [("wo", P_SEG2 + m, m, 0) for m in range(NK)] + weave(
    [("wo", P_SEG2 + NK + m, m, 1) for m in range(NK)],
    {0: both("y", 0), 1: both("n", 0) + both("y", 1), 2: both("n", 1) + both("y", 2),
     3: both("n", 2) + both("y", 3), 4: both("n", 3)}) + weave(
    [("fc1", P_FC1 + m, m, 0) for m in range(4)],
    {0: both("y", 4), 1: both("n", 4) + both("y", 5), 2: both("n", 5) + both("y", 6), 3: both("n", 6)}) + [
    ("logit", 0, 0, 0), ("logit", 0, 0, 1)] + weave(
    [("fc1", P_FC1 + 4 + m, m, 1) for m in range(4)],
    {0: [("logitT",)], 2: [("routing", 0), ("routing", 1)]}) + [
    ("exp", P_EXP + m // 2, m, h) for m in range(4) for h in range(2)] + [
    ("fc2", P_FC2 + m // 2, m, h) for m in range(NK) for h in range(2)]
SEG3 = [("down", P_SEG3 + m, m, 0) for m in range(NK)] + weave(
    [("down", P_SEG3 + NK + m, m, 1) for m in range(NK)],
    {0: both("z", 0), 1: both("z", 1), 2: both("z", 2), 3: both("z", 3)}) + [
    g for r in range(4, RT) for g in both("z", r)]

PRODUCTS = ("q", "wo", "fc1", "exp", "fc2", "down")


def slab_turns(segment):
    turns, last = {}, -1
    for j, g in enumerate(segment):
        if g[0] in PRODUCTS:
            if g[1] not in turns.values():
                turns[last] = g[1]
            last = j
    return turns


C_SEG1 = 0
C_Q2 = C_SEG1 + len(SEG1)
C_Q3 = C_Q2 + 2 * (NH - 2 * EDGE)
C_KV = C_Q3 + len(SEG_Q3)
C_WO = C_KV + 8 * B
C_SEG2 = C_WO + (NKV - 1) * 2 * NK
C_FFN = C_SEG2 + len(SEG2)
C_SEG3 = C_FFN + 3 * 2 * NK

WITH_HI = ("ln", "q", "n", "fc1", "exp")


def hi_before(segment, start):
    out = [start]
    for g in segment:
        out.append(out[-1] + (g[0] in WITH_HI))
    return out


H_SEG1 = hi_before(SEG1, 0)
H_Q2 = H_SEG1[-1]
H_Q3 = hi_before(SEG_Q3, H_Q2 + 2 * (NH - 2 * EDGE))
H_KV = H_Q3[-1]
H_SEG2 = hi_before(SEG2, H_KV + 8 * B)
H_FFN = H_SEG2[-1]
L_FFN = 2 * (LAT // P)


def xattn_ffn(nc, x, ctxT, slabs, wkv, gate, gamma, beta, out):
    with ExitStack() as top:
        def sb(name, cols, dt=F32):
            return top.enter_context(nc.sbuf_tensor(name, [P, cols], dt))

        def sem(name):
            return top.enter_context(nc.semaphore(name))

        def sems(name, n):
            return [sem(f"{name}{j}") for j in range(n)]

        def dram(name, shape):
            return nc.dram_tensor(name, shape, F32).ap()

        xt_d = dram("xt_scratch", (P, 2, NK, ROWS))
        q_d = dram("q_scratch", (NKV, P, 2, G, ROWS))
        k_d = dram("k_scratch", (NKV, B, P, 2 * KP))
        v_d = dram("v_scratch", (NKV, B, KT, 2, 4, D))
        k_f = k_d.rearrange("h b p c -> (h b) p c")
        v_f = v_d.rearrange("h b p l t d -> (h b) p (l t d)")
        x2_d = dram("x2_beta_scratch", (ROWS, HID))

        RA = sb("act_region", 2 * 2 * NK * KP, F32R)
        RB = sb("mid_region", 16384, F32R)
        RC = sb("slab_split", 4 * SLAB, F32R)
        RD = sb("small_region", 2048, F32R)
        RAW = sb("slab_raw", 2 * SLAB)
        FB = sb("tile_region", 4096)
        YR = sb("y_region", NK * ROWS)
        ident = sb("ident", P)
        ones = sb("ones", P)
        gate_raw = sb("gate_raw", NK * NE)
        small = sb("small", 224)

        def part(t, at, n):
            return t[:, at:at + n]

        def f32(ap):
            return ap.bitcast(F32)

        def rows_hl(region, tiles):
            views, at_ = [], 0
            for first, end in PARTS:
                n = tiles * (end - first)
                views.append([part(region, at_ + l * n, n).rearrange("p (k n) -> p k n", k=tiles) for l in range(2)])
                at_ += 2 * n
            return views

        XT = rows_hl(RA, NK)
        AT = [part(RA, l * NK * ROWS, NK * ROWS).rearrange("p (g n) -> p g n", g=G) for l in range(2)]
        HT = [[part(RA, (2 * j + l) * NK * KP, NK * KP).rearrange("p (k n) -> p k n", k=NK)
               for l in range(2)] for j in range(2)]
        IN = rows_hl(RA, NK)
        PIECE = 2 * 512
        WKV = [[part(RB, (2 * j + l) * PIECE, PIECE) for l in range(2)] for j in range(8)]
        at = 0
        QB = [part(RB, at + s * 2 * QC, 2 * QC) for s in range(2)]
        at += 4 * QC
        KB = [part(RB, at + s * 2 * KP, 2 * KP) for s in range(2)]
        at += 4 * KP
        VB = [part(RB, at + s * 8 * D, 8 * D) for s in range(2)]
        assert at + 16 * D <= 8 * PIECE
        PT = [part(RB, 8 * PIECE + l * 4 * QC, 4 * QC).rearrange("p (t n) -> p t n", t=4) for l in range(2)]
        X2 = rows_hl(RB, NK)
        WS = [[part(RC, (2 * s + l) * SLAB, SLAB) for l in range(2)] for s in range(2)]
        KVST = [[part(RD, (2 * s + l) * 512, 512) for l in range(2)] for s in range(2)]
        QSTV = [part(RD, s * 1024, 1024).rearrange("p (l n) -> p l n", l=2) for s in range(2)]
        KVSTV = QSTV
        GT = [part(RD, l * NK * P, NK * P).rearrange("p (k n) -> p k n", k=NK) for l in range(2)]
        RAWS = [part(RAW, s * SLAB, SLAB) for s in range(2)]
        PRAW = [part(FB, j * PIECE, PIECE) for j in range(2)]
        CRAW = part(FB, 0, NK * SC).rearrange("p (k n) -> p k n", k=NK)
        PR = [part(FB, i * KP, KP) for i in range(QT)]
        XIN = [part(FB, s * HID, HID) for s in range(2)]
        XN = part(FB, 2 * HID, HID)
        BETA = part(FB, 3 * HID, HID)
        RWREP = part(FB, 0, ROWS).rearrange("p (r n) -> p r n", r=RT)
        RWB = part(FB, HID, ROWS)
        LGT = part(FB, 2 * HID, ROWS)
        RELU = part(FB, 3 * HID, 512)
        SQT = part(FB, 3 * HID + 512, 512)
        GAMMA = part(FB, 0, HID)
        CEN = [part(FB, (2 + s) * HID, HID) for s in range(2)]
        XB = [part(FB, HID, HID)] + [f32(part(RD, s * HID, HID)) for s in range(2)]
        XB += XB[0:2] + RAWS
        X7 = YR[:, :].rearrange("p (r n) -> p r n", r=RT)
        Y = YR[:, :].rearrange("p (k n) -> p k n", k=NK)
        stats = small[:, 0:12]
        mv = small[:, 16:16 + 2 * RT].rearrange("p (r c) -> p r c", c=2)
        sd = small[:, 32:32 + RT]
        rs = small[:, 40:40 + RT]
        negmax = small[:, 48:48 + QT]
        rowsum = small[:, 56:56 + QT]
        rrow = small[:, 64:64 + QT]
        rw = small[:, 72:72 + RT]
        lg = small[:, 80:80 + RT * NE]
        top8 = small[:, 144:144 + RT * NE]

        bank = [top.enter_context(nc.psum_tensor(f"bank{j}", [P, 512], F32)) for j in range(8)]
        GB = [bank[7], bank[3], bank[4], bank[5]]
        SB, AV = bank[0:3], bank[5:7]
        order = [GB[(C_WO + j) % 4] for j in range(4)]
        LAST_USE = [j for j in range(4) if order[j] is not bank[5]]
        TB = [order[j] for j in LAST_USE]
        LAST_USE.append([j for j in range(4) if order[j] is bank[5]][0])

        RING = [0, 1, 2, 0, 1, 2, 0]
        FREED_BY = [0, 0, 0, 1, 2, 3, 4]

        STATS_AT = {(0, 0): 2, (1, 0): 3, (4, 0): 5, (5, 0): 6}

        def gb(c):
            return GB[c % 4]

        s_x = sems("x_loaded", RT)
        s_raw = sems("slab_loaded", 2)
        s_piece = sems("kv_piece_loaded", 2)
        s_ctx = sem("ctx_loaded")
        s_lat = sems("latents_loaded", 2)
        s_xt = sem("xt_stored")
        s_qst = sems("q_stored", 2)
        s_kvst = sems("kv_stored", 2)
        s_qk = sems("qk_loaded", 2)
        s_v = sems("v_loaded", 2)
        s_xin = sems("x_again", 2)
        s_x2st = sems("x2_stored", 2)
        s_misc = sem("gate_beta_loaded")
        s_gamma = sem("gamma_loaded")
        s_out = sems("out_stored", 2)
        s_const = sem("consts_made")
        s_agg = sem("stats_done")
        s_sd = sem("sd_done")
        s_link = sem("vector_chain")
        s_xn = sem("rows_normalised")
        s_mm = sem("group_done")
        s_hi = sem("hi_of_group")
        s_ev = sem("group_taken")
        s_lo = sem("lo_of_tile")
        s_relu = sem("relu_done")
        s_whi = sem("slab_hi")
        s_wlo = sem("slab_lo")
        s_phi = sem("piece_hi")
        s_plo = sem("piece_lo")
        s_chi = sem("ctx_hi")
        s_clo = sem("ctx_lo")
        s_pad = sem("pad_zeroed")
        s_s = sem("scores_done")
        s_max = sem("max_done")
        s_exp = sem("exp_done")
        s_rec = sem("reciprocal_done")
        s_pn = sem("p_normalised")
        s_t = sem("pT_done")
        s_pth = sem("pT_hi")
        s_ptl = sem("pT_lo")
        s_av = sem("av_done")
        s_avh = sem("av_hi")
        s_avl = sem("av_lo")
        s_zero = sem("y_zeroed")
        s_gz = sem("gate_zeroed")
        s_gs = sem("gate_split")
        s_x2 = sem("x2_summed")
        s_x2b = sem("x2_beta")
        s_rw = sem("routing_weight")
        s_o = sem("out_tile")

        top.enter_context(nc.allow_non_contiguous_dma(reason="scratch rows of 448 bytes"))
        block = top.enter_context(nc.Block())

        def piece(j, l):
            return RB[:, bass.ds((2 * j + l) * PIECE, PIECE)]

        def row_tile(xt, l, r, h):
            return xt[r // 4][l][:, 4 * h:4 * h + 4, (r % 4) * P:(r % 4 + 1) * P]

        @block.sync
        def _(sp):
            def load_slab(p, s, slab):
                sp.wait_ge(s_wlo, p - 1)
                sp.dma_start(RAWS[s], slabs[slab]).then_inc(s_raw[s], 16)

            def next_slab(p):
                if p + 2 < N_POS:
                    load_slab(p + 2, p % 2, SLAB_AT[p + 2])

            def next_slabs(p0, n):
                assert SLAB_AT[p0 + 2:p0 + n + 2] == list(range(SLAB_AT[p0 + 2], SLAB_AT[p0 + 2] + n))
                with sp.Fori(0, n // 2) as i:
                    for s in range(2):
                        load_slab(p0 + 2 + 2 * i + s, s, SLAB_AT[p0 + 2] + 2 * i + s)

            for r in range(RT):
                sp.dma_start(X7[:, r, :], x[r * P:(r + 1) * P, :]).then_inc(s_x[r], 16)
                if r in (3, 5):
                    s = (r - 3) // 2
                    sp.dma_start(RAWS[s], slabs[s]).then_inc(s_raw[s], 16)
            for j in range(2):
                sp.dma_start(PRAW[j], wkv[j]).then_inc(s_piece[j], 16)

            def store_q(kv, g, h, c, slot):
                sp.wait_ge(s_ev, c + 1)
                first, end = PARTS[h]
                sp.dma_start(q_d[kv, :, :, g, first:end],
                             f32(QSTV[slot][:, :, 0:end - first])).then_inc(s_qst[slot], 16)

            def store_q_of(segment, c0, p):
                for j, g in enumerate(segment):
                    if g[0] == "q" and g[1] == p:
                        store_q(g[2] // G, g[2] % G, g[3], c0 + j, g[1] % 2)

            next_slab(0)
            for p in range(2 * EDGE):
                if p + 1 < 2 * EDGE:
                    next_slab(p + 1)
                store_q_of(SEG1, C_SEG1, p)

            def q_position(p, s, m_hi, m_lo, c):
                load_slab(p + 2, s, p + 2 - EDGE)
                for h in range(2):
                    store_q(m_hi, m_lo, h, c + h, h)

            def q_heads(kv, first, n):
                for g in range(first, first + n):
                    m = kv * G + g
                    q_position(m + EDGE, g % 2, kv, g, C_Q2 + 2 * (m - EDGE))

            q_heads(0, EDGE, G - EDGE)
            with sp.Fori(1, NKV - 1) as kv:
                q_heads(kv, 0, G)
            sp.wait_ge(s_plo, NK)
            sp.dma_start(CRAW, ctxT[0]).then_inc(s_ctx, 16)
            q_heads(NKV - 1, 0, EDGE - 2)
            for g in range(EDGE - 2, G - EDGE):
                m = (NKV - 1) * G + g
                next_slab(m + EDGE)
                for h in range(2):
                    store_q(NKV - 1, g, h, C_Q2 + 2 * (m - EDGE) + h, h)

            def latents(b, j):
                for l in range(2):
                    sp.dma_start(f32(HT[j][l][:, :, SC:KEYS]), xt_d[:, l, :, bass.ds(b * SQ, SQ)]).then_inc(s_lat[j], 16)

            next_slab(P_Q3)
            for p in range(P_Q3, P_WO):
                if p + 1 < P_WO:
                    next_slab(p + 1)
                if p == P_Q3 + EDGE:
                    sp.wait_ge(s_mm, C_Q3 + EDGE)
                    sp.wait_ge(s_xt, XT_STORED)
                    latents(0, 0)
                store_q_of(SEG_Q3, C_Q3, p)

            def load_qk(kv, b, n, s):
                for l in range(2):
                    sp.dma_start(f32(QB[s])[:, l * QC:(l + 1) * QC].rearrange("p (g c) -> p g c", g=G),
                                 q_d[kv, :, l, :, bass.ds(b * SQ, SQ)]).then_inc(s_qk[s], 16)
                sp.dma_start(f32(KB[s]), k_f[n]).then_inc(s_qk[s], 16)

            def load_v(n, s):
                sp.dma_start(f32(VB[s])[0:KT, :], v_f[n]).then_inc(s_v[s], 16)

            def kv_batch(b, j, more):
                if more:
                    sp.wait_ge(s_mm, C_KV + 8 * b)
                    latents(b + 1, 1 - j)
                    sp.wait_ge(s_clo, b + 1)
                    sp.dma_start(CRAW, ctxT[b + 1]).then_inc(s_ctx, 16)
                for u in range(8):
                    s = u % 2
                    sp.wait_ge(s_ev, C_KV + 8 * b + u + 1)
                    if u < 4:
                        sp.dma_start(k_d[u, b].rearrange("p (l c) -> p l c", l=2),
                                     f32(KVSTV[s][:, :, 0:KP])).then_inc(s_kvst[s], 16)
                    else:
                        for l in range(2):
                            sp.dma_start(v_d[:, b, :, l, u - 4, :].rearrange("h p d -> p h d"),
                                         f32(KVST[s][l])[0:KT, :].rearrange("p (h d) -> p h d", h=NKV)
                                         ).then_inc(s_kvst[s], 16)
                    if not more and u == 3:
                        sp.wait_ge(s_mm, C_WO - 4)
                    if not more and u in (3, 5):
                        load_qk(0, u // 4, u // 4, u // 4)
                    if not more and u == 7:
                        for n in range(2):
                            load_v(n, n)

            with sp.Fori(0, B // 2 - 1) as i:
                for j in range(2):
                    kv_batch(2 * i + j, j, True)
            kv_batch(B - 2, 0, True)
            for s in range(2):
                sp.wait_ge(s_qst[s], FREE + 16 * NH)
                sp.wait_ge(s_kvst[s], FREE + 16 * (B - 1) * (2 + 4))
            kv_batch(B - 1, 1, False)
            for s in range(2):
                sp.wait_ge(s_kvst[s], FREE + 16 * B * (2 + 4))

            def attention_loads(kv, b, n, s):
                sp.wait_ge(s_s, QT * n)
                load_qk(kv, b, n + 1, 1 - s)
                sp.wait_ge(s_av, 2 * n)
                load_v(n + 1, 1 - s)

            def loads_of_steps(kv, b0, n_steps):
                with sp.Fori(0, n_steps // 2) as i:
                    for j in range(2):
                        b = b0 + 2 * i + j
                        attention_loads(kv, b + 2, kv * B + b + 1, 1 - j)

            with sp.Fori(0, NKV - 1) as kv:
                loads_of_steps(kv, 0, B - 2)
                for j in range(2):
                    attention_loads(kv + 1, j, kv * B + B - 1 + j, 1 - j)
                with sp.Fori(0, NK // 2) as i:
                    for s in range(2):
                        p = P_WO + 2 + kv * NK + 2 * i + s
                        load_slab(p, s, T_WO + 2 + kv * NK + 2 * i + s)
            loads_of_steps(NKV - 1, 0, B - 2)
            sp.wait_ge(s_t, QT * NKV * B)
            sp.dma_start(BETA, beta.partition_broadcast(P)).then_inc(s_misc, 16)
            sp.dma_start(gate_raw[:, :], gate).then_inc(s_misc, 16)
            for s in range(2):
                sp.dma_start(XIN[s], x[s * P:(s + 1) * P, :]).then_inc(s_xin[s], 16)

            turns = slab_turns(SEG2)
            next_slab(P_SEG2)
            for j, g in enumerate(SEG2):
                if j in turns:
                    next_slab(turns[j])
                if g[0] == "n" and g[2] == 1:
                    r = g[1]
                    sp.wait_ge(s_x2b, r + 1)
                    sp.dma_start(x2_d[r * P:(r + 1) * P, :], XIN[r % 2]).then_inc(s_x2st[r % 2], 16)
                if g[0] == "y" and g[2] == 1 and 1 <= g[1] < RT - 1:
                    r = g[1] - 1
                    sp.wait_ge(s_x2st[r % 2], 16 * (r // 2 + 1))
                    sp.dma_start(XIN[r % 2], x[(r + 2) * P:(r + 3) * P, :]).then_inc(s_xin[r % 2], 16)

            def load_x2(r):
                sp.dma_start(XB[r], x2_d[r * P:(r + 1) * P, :]).then_inc(s_xin[r % 2], 16)

            for s in range(2):
                sp.wait_ge(s_x2st[s], 16 * ((RT + 1 - s) // 2))
            sp.wait_ge(s_lo, L_FFN)
            sp.dma_start(GAMMA, gamma.partition_broadcast(P)).then_inc(s_gamma, 16)
            for r in range(3):
                load_x2(r)
            next_slabs(P_FFN, 3 * NK)

            def store_out(r):
                sp.wait_ge(s_o, r + 1)
                sp.dma_start(out[r * P:(r + 1) * P, :], CEN[r % 2]).then_inc(s_out[r % 2], 16)
                if r < 2:
                    load_x2(r + 3)

            turns = slab_turns(SEG3)
            next_slab(P_SEG3)
            for j, g in enumerate(SEG3):
                if j in turns:
                    next_slab(turns[j])
                    if g[3] == 1 and 1 <= g[2] <= 4:
                        store_out(g[2] - 1)
                if g == ("z", 4, 0):
                    for r in (5, 6):
                        sp.wait_ge(s_wlo, N_POS + r - 6)
                        load_x2(r)
            for r in range(4, RT):
                store_out(r)
            for s in range(2):
                sp.wait_ge(s_out[s], 16 * ((RT + 1 - s) // 2))

        @block.gpsimd
        def _(pool):
            pool.memset(ident[:, :], 0.0).then_inc(s_const, 1)
            pool.memset(ones[:, :], 1.0).then_inc(s_const, 1)
            pool.wait_ge(s_const, 2)
            pool.affine_select(out=ident[:, :], in_=ident[:, :], compare_op=ALU.not_equal, fill=1.0, base=0,
                               pattern=[[-1, P]], channel_multiplier=1).then_inc(s_const, 1)

            for n, (free, count) in enumerate([*((q, FREE) for q in (*s_qst, *s_kvst)), (s_avl, 2)]):
                pool.memset(small[:, 212 + n:213 + n], 0.0).then_inc(free, count)

            def slab_lo(p, s):
                pool.wait_ge(s_whi, p + 1)
                pool.tensor_tensor(WS[s][1], RAWS[s], f32(WS[s][0]), ALU.subtract).then_inc(s_wlo, 1)

            def slabs_lo(p0, n):
                with pool.Fori(0, n // 2) as i:
                    for j in range(2):
                        slab_lo(p0 + 2 * i + j, 1 - j)

            def zero_pad(j):
                for l in range(2):
                    pool.memset(f32(HT[j][l][:, :, KEYS:KP]), 0.0).then_inc(s_pad, 1)

            def ctx_lo(b, j):
                pool.wait_ge(s_chi, b + 1)
                pool.tensor_tensor(HT[j][1][:, :, 0:SC], CRAW, f32(HT[j][0][:, :, 0:SC]),
                                   ALU.subtract).then_inc(s_clo, 1)

            slab_lo(0, 0)
            slabs_lo(1, P_Q3 + EDGE)
            slab_lo(P_Q3 + EDGE + 1, 1)
            pool.wait_ge(s_mm, C_Q3 + EDGE)
            pool.wait_ge(s_xt, XT_STORED)
            zero_pad(0)
            for p in range(P_Q3 + EDGE + 2, P_WO + 1):
                slab_lo(p, p % 2)
            pool.wait_ge(s_mm, C_KV)
            zero_pad(1)
            ctx_lo(1, 1)
            with pool.Fori(1, B // 2) as i:
                for j in range(2):
                    ctx_lo(2 * i + j, j)
            pool.wait_ge(s_ev, C_SEG1 + len(SEG1))
            pool.memset(YR[:, :], 0.0).then_inc(s_zero, 1)
            pool.wait_ge(s_clo, B)
            pool.memset(FB[:, 0:QT * KP].rearrange("p (i c) -> p i c", i=QT)[:, :, KEYS:KP], 0.0).then_inc(s_zero, 1)

            def p_normalise(n):
                for i in range(QT):
                    pool.wait_ge(s_rec, QT * n + i + 1)
                    pool.tensor_tensor(PR[i], PR[i], rrow[:, i:i + 1].broadcast_to([P, KP]),
                                       ALU.mult).then_inc(s_pn, 1)

            p_normalise(0)
            for s in range(2):
                pool.wait_ge(s_kvst[s], FREE + 16 * B * (2 + 4))
            pool.memset(f32(RD[:, :]), 0.0).then_inc(s_gz, 1)
            with pool.Fori(0, NKV - 1) as kv:
                with pool.Fori(0, B) as i:
                    p_normalise(kv * B + i + 1)
                slabs_lo(P_WO + 1 + kv * NK, NK)
            with pool.Fori(0, B - 1) as i:
                p_normalise((NKV - 1) * B + i + 1)
            pool.wait_ge(s_misc, 32)
            turns = slab_turns(SEG2)
            slab_lo(P_SEG2 + 1, 1)
            for j, g in enumerate(SEG2):
                if j in turns:
                    slab_lo(turns[j] + 1, (turns[j] + 1) % 2)
                if g[0] == "y" and g[2] == 1:
                    r = g[1]
                    pool.wait_ge(s_xn, RT + r + 1)
                    pool.tensor_tensor(XIN[r % 2], XIN[r % 2], BETA, ALU.add).then_inc(s_x2b, 1)
            slabs_lo(P_FFN + 1, N_POS - P_FFN - 2)
            slab_lo(N_POS - 1, 1)

        @block.scalar
        def _(act):
            def slab_hi(p, s, c):
                act.wait_ge(s_raw[s], 8 * p + 16 - 8 * s)
                act.wait_ge(s_mm, c)
                act.activation(WS[s][0], RAWS[s], ACT.Copy).then_inc(s_whi, 1)

            def next_hi(p0, n, c0):
                with act.Fori(0, n // 2) as i:
                    for s in range(2):
                        slab_hi(p0 + 1 + 2 * i + s, 1 - s, c0 + 4 * i + 2 * s)

            def hi(c, dst, src, scale=1.0):
                act.wait_ge(s_mm, c + 1)
                act.activation(dst, src, ACT.Copy, scale=scale).then_inc(s_hi, 1)

            def sqrt_var(r, n):
                act.wait_ge(s_agg, n + 1)
                act.activation(sd[:, r:r + 1], mv[:, r, 1:2], ACT.Sqrt, bias=eps_ap).then_inc(s_sd, 1)

            def rows_hi(xt, r, h, c):
                hi(c, row_tile(xt, 0, r, h), gb(c)[:, :].rearrange("p (k n) -> p k n", k=4))

            def q_hi(c, c_static, h, slot, freed):
                act.wait_ge(s_qst[slot], FREE + freed)
                n = PARTS[h][1] - PARTS[h][0]
                hi(c, QSTV[slot][:, 0, 0:n], gb(c_static)[:, 0:n], SCALE)

            eps_ap = small[:, 208:209]
            act.wait_ge(s_link, 1)
            turns = slab_turns(SEG1)
            for r in range(2):
                sqrt_var(r, r)
            for j, g in enumerate(SEG1):
                c = C_SEG1 + j
                if g[0] == "ln":
                    _, r, h = g
                    if (r, h) in STATS_AT:
                        sqrt_var(STATS_AT[r, h], STATS_AT[r, h])
                    rows_hi(XT, r, h, c)
                    if (r, h) == (3, 1):
                        sqrt_var(4, 4)
                    if r == 1 and h == 1:
                        slab_hi(0, 0, c)
                else:
                    _, p, m, h = g
                    if p == 0:
                        slab_hi(1, 1, c)
                    q_hi(c, c, h, p % 2, 16 * (p // 2))
                    if j in turns:
                        slab_hi(turns[j] + 1, (turns[j] + 1) % 2, c + 1)

            def q_positions(i):
                for s in range(2):
                    c = C_Q2 + 4 * i + 2 * s
                    slab_hi(P_Q2 + 2 * i + s + 1, 1 - s, c)
                    for h in range(2):
                        q_hi(c + h, C_Q2 + 2 * s + h, h, h, 16 * EDGE + 32 * i + 16 * s)

            def q_with_piece(i, j, more):
                k = 2 * i + j
                act.wait_ge(s_piece[j], 16 * (i + 1))
                act.activation(piece(k, 0), PRAW[j], ACT.Copy).then_inc(s_phi, 1)
                for h, (first, end) in enumerate(PARTS):
                    for l in range(2):
                        act.dma_start(xt_d[:, l, k, first:end], f32(XT[h][l][:, k, :])).then_inc(s_xt, 16)
                q_positions(k)
                if more:
                    act.wait_ge(s_plo, k + 1)
                    act.dma_start(PRAW[j], wkv[k + 2]).then_inc(s_piece[j], 16)

            act.wait_ge(s_ev, C_Q2)
            with act.Fori(0, NK // 2 - 1) as i:
                for j in range(2):
                    q_with_piece(i, j, True)
            for j in range(2):
                q_with_piece(NK // 2 - 1, j, False)
            with act.Fori(NK, (NH - 2 * EDGE) // 2) as i:
                q_positions(i)

            def ctx_hi(b, j, c):
                act.wait_ge(s_ctx, 16 * (b + 1))
                act.wait_ge(s_mm, c)
                act.activation(HT[j][0][:, :, 0:SC], CRAW, ACT.Copy).then_inc(s_chi, 1)

            for j, g in enumerate(SEG_Q3):
                _, p, m, h = g
                c = C_Q3 + j
                slab_hi(p + 1, (p + 1) % 2, c)
                if j == EDGE:
                    act.wait_ge(s_xt, XT_STORED)
                    ctx_hi(0, 0, c)
                q_hi(c, c, h, p % 2, 16 * (NH - EDGE + (j // 2)))

            def kv_hi(b, j, before, more):
                if more:
                    ctx_hi(b + 1, 1 - j, C_KV + 8 * b)
                for u in range(8):
                    s, c = u % 2, C_KV + u
                    p, n = (P, KP) if u < 4 else (KT, 512)
                    act.wait_ge(s_kvst[s], FREE + before + [0, 0, 16, 16, 32, 32, 64, 64][u])
                    hi(C_KV + 8 * b + u, KVST[s][0][0:p, 0:n], gb(c)[0:p, 0:n])

            for s in range(2):
                act.wait_ge(s_qst[s], FREE + 16 * NH)
            act.wait_ge(s_link, 1)
            act.activation(small[:, 209:210], eps_ap, ACT.Exp)
            with act.Fori(0, B // 2 - 1) as i:
                for j in range(2):
                    kv_hi(2 * i + j, j, (2 * i + j) * 96, True)
            kv_hi(B - 2, 0, (B - 2) * 96, True)
            kv_hi(B - 1, 1, (B - 1) * 96, False)

            def exp(n, i):
                act.wait_ge(s_max, QT * n + i + 1)
                act.activation(PR[i][:, 0:KEYS], SB[RING[i]][:, 0:KEYS], ACT.Exp, bias=negmax[:, i:i + 1],
                               accum_out=rowsum[:, i:i + 1]).then_inc(s_exp, 1)

            def attention(n, b, scores, av):
                for i in range(QT):
                    if av:
                        act.wait_ge(s_t, QT * (n - 1) + i + 1)
                        act.activation(PT[0][0:KT, :, i * P:(i + 1) * P],
                                       TB[RING[i]][0:KT, :].rearrange("p (t n) -> p t n", t=4),
                                       ACT.Copy).then_inc(s_pth, 1)
                    if scores and i >= 1:
                        exp(n, i - 1)
                if scores:
                    exp(n, QT - 1)
                if av:
                    for a in range(2):
                        act.wait_ge(s_av, 2 * (n - 1) + a + 1)
                        act.activation(AT[0][:, 4 * a:4 * a + 4, bass.ds(b * SQ, SQ)],
                                       AV[a][:, 0:QH].rearrange("p (g n) -> p g n", g=4), ACT.Copy).then_inc(s_avh, 1)

            act.wait_ge(s_zero, 2)
            attention(0, 0, True, False)
            with act.Fori(0, NKV - 1) as kv:
                with act.Fori(0, B) as b:
                    attention(kv * B + b + 1, b, True, True)
                next_hi(P_WO + kv * NK, NK, C_WO + kv * 2 * NK)
            with act.Fori(0, B - 1) as b:
                attention((NKV - 1) * B + b + 1, b, True, True)
            attention(NKV * B, B - 1, False, True)

            act.activation(small[:, 210:211], eps_ap, ACT.Sqrt)
            act.wait_ge(s_misc, 32)
            act.wait_ge(s_gz, 1)
            act.activation(GT[0][:, :, 0:NE], gate_raw[:, :].rearrange("p (k e) -> p k e", k=NK),
                           ACT.Copy).then_inc(s_phi, 1)
            turns = slab_turns(SEG2)
            slab_hi(P_SEG2 + 1, 1, C_SEG2)
            for j, g in enumerate(SEG2):
                c, what = C_SEG2 + j, g[0]
                if what == "y" and g[2] == 1:
                    sqrt_var(g[1], RT + g[1])
                if what == "n":
                    rows_hi(X2, g[1], g[2], c)
                if what == "fc1":
                    n = PARTS[g[3]][1] - PARTS[g[3]][0]
                    hi(c, IN[g[3]][0][:, g[2], :], gb(c)[:, 0:n])
                if what == "exp":
                    n = PARTS[g[3]][1] - PARTS[g[3]][0]
                    act.wait_ge(s_ev, c + 1)
                    act.activation(IN[g[3]][0][:, 4 + g[2], :], SQT[:, 0:n], ACT.Copy).then_inc(s_hi, 1)
                if j in turns:
                    slab_hi(turns[j] + 1, (turns[j] + 1) % 2, c + 1)

            def up(p0, c0):
                with act.Fori(0, NK // 2) as i:
                    for s in range(2):
                        m = 2 * i + s
                        slab_hi(p0 + 1 + m, 1 - s, c0 + 2 * m)
                        for h, (first, end) in enumerate(PARTS):
                            c, n = c0 + 2 * m + h, end - first
                            act.wait_ge(s_mm, c + 1)
                            act.activation(RELU[:, 0:n], gb(C_FFN + 2 * s + h)[:, 0:n], ACT.Relu).then_inc(s_relu, 1)
                            act.wait_ge(s_ev, c + 1)
                            act.activation(IN[h][0][:, m, :], SQT[:, 0:n], ACT.Copy).then_inc(s_hi, 1)

            up(P_FFN, C_FFN)
            next_hi(P_FFN + NK, NK, C_FFN + 2 * NK)
            up(P_FFN + 2 * NK, C_FFN + 4 * NK)

            turns = slab_turns(SEG3)
            slab_hi(P_SEG3 + 1, 1, C_SEG3)
            for j, g in enumerate(SEG3):
                if j in turns and turns[j] + 1 < N_POS:
                    slab_hi(turns[j] + 1, (turns[j] + 1) % 2, C_SEG3 + j + 1)
                if g[0] == "z" and g[2] == 1:
                    sqrt_var(g[1], 2 * RT + g[1])

        @block.vector
        def _(dve):
            chain = [0]

            def link(ins):
                chain[0] += 1
                ins.then_inc(s_link, 1)
                dve.wait_ge(s_link, chain[0])

            def lo(c, h, dst, src, hi_of):
                dve.wait_ge(s_hi, h + 1)
                dve.tensor_tensor(dst, src, f32(hi_of), ALU.subtract).then_inc(s_ev, 1)

            def rows_lo(xt, r, h, c, nh):
                lo(c, nh, row_tile(xt, 1, r, h), gb(c)[:, :].rearrange("p (k n) -> p k n", k=4), row_tile(xt, 0, r, h))

            def mean_var(r, n, halves):
                for h in range(2):
                    ins = dve.bn_stats(stats[:, 6 * h:6 * h + 6], halves[h])
                link(ins)
                dve.bn_aggr(mv[:, r, :], stats).then_inc(s_agg, 1)
                dve.wait_ge(s_agg, n + 1)

            def reciprocal_sd(r, n):
                dve.wait_ge(s_sd, n + 1)
                link(dve.reciprocal(rs[:, r:r + 1], sd[:, r:r + 1]))

            def normalise(r, n, dst, src):
                reciprocal_sd(r, n)
                dve.tensor_scalar(dst, src, mv[:, r, 0:1], rs[:, r:r + 1], ALU.subtract, ALU.mult).then_inc(s_xn, 1)

            link(dve.memset(small[:, 208:209], EPS))

            def q_lo(nh, c_static, h, slot):
                n = PARTS[h][1] - PARTS[h][0]
                dve.wait_ge(s_hi, nh + 1)
                dve.scalar_tensor_tensor(out=QSTV[slot][:, 1, 0:n], in0=gb(c_static)[:, 0:n], scalar=SCALE,
                                         in1=f32(QSTV[slot][:, 0, 0:n]), op0=ALU.mult, op1=ALU.subtract).then_inc(s_ev, 1)

            def x_stats(r):
                dve.wait_ge(s_x[r], 16)
                mean_var(r, r, [X7[:, r, 0:512], X7[:, r, 512:1024]])

            for r in range(2):
                x_stats(r)
            normalise(0, 0, X7[:, 0, :], X7[:, 0, :])
            for j, g in enumerate(SEG1):
                c = C_SEG1 + j
                if g[0] == "ln":
                    _, r, h = g
                    if (r, h) in STATS_AT:
                        x_stats(STATS_AT[r, h])
                    if h == 0 and r + 1 < RT and r != 3:
                        normalise(r + 1, r + 1, X7[:, r + 1, :], X7[:, r + 1, :])
                    rows_lo(XT, r, h, c, H_SEG1[j])
                    if (r, h) == (3, 1):
                        x_stats(4)
                        normalise(4, 4, X7[:, 4, :], X7[:, 4, :])
                else:
                    _, p, m, h = g
                    q_lo(H_SEG1[j], c, h, p % 2)

            def q_positions(i):
                for s in range(2):
                    for h in range(2):
                        q_lo(H_Q2 + 4 * i + 2 * s + h, C_Q2 + 2 * s + h, h, h)

            with dve.Fori(0, NK // 2) as i:
                for j in range(2):
                    k = 2 * i + j
                    dve.wait_ge(s_phi, k + 1)
                    dve.tensor_tensor(piece(k, 1), PRAW[j], f32(piece(k, 0)), ALU.subtract).then_inc(s_plo, 1)
                    q_positions(k)
            with dve.Fori(NK, (NH - 2 * EDGE) // 2) as i:
                q_positions(i)
            for j, g in enumerate(SEG_Q3):
                q_lo(H_Q3[j], C_Q3 + j, g[3], g[1] % 2)
                if j == EDGE:
                    dve.wait_ge(s_chi, 1)
                    dve.tensor_tensor(HT[0][1][:, :, 0:SC], CRAW, f32(HT[0][0][:, :, 0:SC]),
                                      ALU.subtract).then_inc(s_clo, 1)

            with dve.Fori(0, B) as b:
                for u in range(8):
                    s = u % 2
                    p, n = (P, KP) if u < 4 else (KT, 512)
                    lo(None, H_KV + 8 * b + u, KVST[s][1][0:p, 0:n], gb(C_KV + u)[0:p, 0:n], KVST[s][0][0:p, 0:n])

            def reciprocal_sums(n, first, end):
                dve.wait_ge(s_exp, QT * n + end)
                dve.reciprocal(rrow[:, first:end], rowsum[:, first:end]).then_inc(s_rec, end - first)

            def max_of(n, i):
                dve.wait_ge(s_s, QT * n + i + 1)
                dve.reduce_max(negmax[:, i:i + 1], SB[RING[i]][:, 0:KEYS], AX.X, negate=True).then_inc(s_max, 1)

            def av_lo(n, b, a):
                dve.wait_ge(s_avh, 2 * n + a + 1)
                at_ = (slice(None), slice(4 * a, 4 * a + 4), bass.ds(b * SQ, SQ))
                dve.tensor_tensor(AT[1][at_], AV[a][:, 0:QH].rearrange("p (g n) -> p g n", g=4),
                                  f32(AT[0][at_]), ALU.subtract).then_inc(s_avl, 1)

            def attention(n, b, scores, av, pending=True):
                for i in range(QT):
                    if scores and i < QT - 1:
                        max_of(n, i)
                    if av and pending and i == QT - 1:
                        av_lo(n - 2, b - 1, 1)
                    if av:
                        dve.wait_ge(s_pth, QT * (n - 1) + i + 1)
                        cols = slice(i * P, (i + 1) * P)
                        dve.tensor_tensor(PT[1][0:KT, :, cols], TB[RING[i]][0:KT, :].rearrange("p (t n) -> p t n", t=4),
                                          f32(PT[0][0:KT, :, cols]), ALU.subtract).then_inc(s_ptl, 1)
                    if scores and i == 6:
                        reciprocal_sums(n, 0, 4)
                if scores:
                    max_of(n, QT - 1)
                    reciprocal_sums(n, 4, QT)
                if av:
                    av_lo(n - 1, b, 0)

            def add_to_y(c, c_static, m, h):
                dve.wait_ge(s_mm, c + 1)
                cols = slice(*PARTS[h])
                dve.tensor_tensor(Y[:, m, cols], Y[:, m, cols], gb(c_static)[:, 0:PARTS[h][1] - PARTS[h][0]],
                                  ALU.add).then_inc(s_ev, 1)

            def y_slabs(c0, c_static):
                with dve.Fori(0, NK // 2) as i:
                    for s in range(2):
                        for h in range(2):
                            add_to_y(c0 + 4 * i + 2 * s + h, c_static + 2 * s + h, 2 * i + s, h)

            dve.wait_ge(s_zero, 2)
            attention(0, 0, True, False)
            with dve.Fori(0, NKV - 1) as kv:
                attention(kv * B + 1, 0, True, True, False)
                with dve.Fori(1, B) as b:
                    attention(kv * B + b + 1, b, True, True)
                av_lo(kv * B + B - 1, B - 1, 1)
                y_slabs(C_WO + kv * 2 * NK, C_WO)
            attention((NKV - 1) * B + 1, 0, True, True, False)
            with dve.Fori(1, B - 1) as b:
                attention((NKV - 1) * B + b + 1, b, True, True)
            attention(NKV * B, B - 1, False, True)
            av_lo(NKV * B - 1, B - 1, 1)

            dve.wait_ge(s_phi, 9)
            dve.tensor_tensor(GT[1][:, :, 0:NE], gate_raw[:, :].rearrange("p (k e) -> p k e", k=NK),
                              f32(GT[0][:, :, 0:NE]), ALU.subtract).then_inc(s_gs, 1)

            def x2_tile(c, r, h):
                cols = slice(512 * h, 512 * h + 512)
                dve.wait_ge(s_mm, c + 1)
                if h == 0:
                    dve.wait_ge(s_xin[r % 2], 16 * (r // 2 + 1))
                dve.tensor_tensor(XIN[r % 2][:, cols], XIN[r % 2][:, cols], gb(c)[:, :], ALU.add).then_inc(s_ev, 1)
                if h == 1:
                    dve.wait_ge(s_ev, c + 1)
                    mean_var(r, RT + r, [XIN[r % 2][:, 0:512], XIN[r % 2][:, 512:1024]])
                    normalise(r, RT + r, XN, XIN[r % 2])

            def routing_weights(c):
                dve.tensor_copy(lg, gb(c)[:, 0:RT * NE]).then_inc(s_ev, 1)
                dve.wait_ge(s_ev, c + 1)
                for r in range(RT):
                    ins = dve.max(top8[:, r * NE:(r + 1) * NE], lg[:, r * NE:(r + 1) * NE])
                link(ins)
                best = top8.rearrange("p (r e) -> p r e", e=NE)
                link(dve.tensor_tensor(rw.rearrange("p (r e) -> p r e", e=1), best[:, :, 0:1], best[:, :, 1:2], ALU.add))
                for s in range(2):
                    dve.wait_ge(s_x2st[s], 16 * ((RT + 1 - s) // 2))
                for r in range(RT):
                    dve.tensor_scalar(RWREP[:, r, :], ones[:, :], rw[:, r:r + 1], None, ALU.mult).then_inc(s_rw, 1)

            n_lo = 0
            for j, g in enumerate(SEG2):
                c, what = C_SEG2 + j, g[0]
                if len(g) == 4:
                    h, n, cols = g[3], PARTS[g[3]][1] - PARTS[g[3]][0], slice(*PARTS[g[3]])
                if what == "wo":
                    add_to_y(c, c, g[2], h)
                elif what == "y":
                    x2_tile(c, g[1], g[2])
                elif what == "n":
                    rows_lo(X2, g[1], g[2], c, H_SEG2[j])
                elif what == "fc1":
                    lo(c, H_SEG2[j], IN[h][1][:, g[2], :], gb(c)[:, 0:n], IN[h][0][:, g[2], :])
                elif what == "logit":
                    dve.wait_ge(s_mm, c + 1)
                    dve.tensor_copy(LGT[0:NE, cols], gb(c)[0:NE, 0:n]).then_inc(s_ev, 1)
                elif what == "logitT":
                    dve.wait_ge(s_mm, c + 1)
                    routing_weights(c)
                elif what == "routing":
                    cols = slice(*PARTS[g[1]])
                    dve.wait_ge(s_mm, c + 1)
                    dve.tensor_copy(RWB[:, cols], gb(c)[:, 0:cols.stop - cols.start]).then_inc(s_ev, 1)
                elif what == "exp":
                    dve.wait_ge(s_mm, c + 1)
                    dve.wait_ge(s_ev, c)
                    if n_lo:
                        dve.wait_ge(s_lo, n_lo)
                    dve.tensor_tensor(SQT[:, 0:n], gb(c)[:, 0:n], RWB[:, cols], ALU.mult).then_inc(s_ev, 1)
                    dve.wait_ge(s_hi, H_SEG2[j] + 1)
                    dve.tensor_tensor(IN[h][1][:, 4 + g[2], :], SQT[:, 0:n], f32(IN[h][0][:, 4 + g[2], :]),
                                      ALU.subtract).then_inc(s_lo, 1)
                    n_lo += 1
                elif what == "fc2":
                    dve.wait_ge(s_mm, c + 1)
                    dve.tensor_copy(Y[:, g[2], cols], gb(c)[:, 0:n]).then_inc(s_ev, 1)

            def up(f):
                with dve.Fori(0, NK // 2) as i:
                    for s in range(2):
                        for h, (first, end) in enumerate(PARTS):
                            n, w = f * 2 * NK + 4 * i + 2 * s + h, end - first
                            dve.wait_ge(s_lo, L_FFN + n)
                            dve.wait_ge(s_relu, n + 1)
                            dve.scalar_tensor_tensor(out=SQT[:, 0:w], in0=gb(C_FFN + 2 * s + h)[:, 0:w], scalar=0.0,
                                                     in1=RELU[:, 0:w], op0=ALU.max, op1=ALU.mult).then_inc(s_ev, 1)
                            dve.wait_ge(s_hi, H_FFN + n + 1)
                            dve.tensor_tensor(IN[h][1][:, 2 * i + s, :], SQT[:, 0:w], f32(IN[h][0][:, 2 * i + s, :]),
                                              ALU.subtract).then_inc(s_lo, 1)

            up(0)
            y_slabs(C_FFN + 2 * NK, C_FFN)
            up(1)

            dve.wait_ge(s_gamma, 16)

            def z_stats(c, r):
                dve.wait_ge(s_mm, c + 2)
                mean_var(r, 2 * RT + r, [gb(c)[:, :], gb(c + 1)[:, :]])

            def z_out(c, r):
                s = r % 2
                reciprocal_sd(r, 2 * RT + r)
                if r >= 2:
                    dve.wait_ge(s_out[s], 16 * (r // 2))
                for h in range(2):
                    cols = slice(512 * h, 512 * h + 512)
                    dve.scalar_tensor_tensor(out=CEN[s][:, cols], in0=gb(c + h)[:, :], scalar=mv[:, r, 0:1],
                                             in1=GAMMA[:, cols], op0=ALU.subtract, op1=ALU.mult).then_inc(s_ev, 1)
                dve.wait_ge(s_ev, c + 2)
                dve.wait_ge(s_xin[s], 16 * ((RT + 1 - s) // 2 + r // 2 + 1))
                dve.scalar_tensor_tensor(out=CEN[s], in0=CEN[s], scalar=rs[:, r:r + 1], in1=XB[r],
                                         op0=ALU.mult, op1=ALU.add).then_inc(s_o, 1)

            for j, g in enumerate(SEG3):
                c = C_SEG3 + j
                if g[0] == "down":
                    add_to_y(c, c, g[2], g[3])
                elif g[2] == 0:
                    r = g[1]
                    z_stats(c, r)
                    if r >= 5:
                        z_out(c - 2, r - 1)
                    if r < 4 or r == RT - 1:
                        z_out(c, r)

        @block.tensor
        def _(pe):
            def bank_free(c):
                pe.wait_ge(s_ev, c - 3)

            def three(out_ap, w, a, first, last):
                pe.matmul(out_ap, w[0], a[0], start=first, stop=False)
                pe.matmul(out_ap, w[0], a[1], start=False, stop=False)
                return pe.matmul(out_ap, w[1], a[0], start=False, stop=last)

            def product(s, acts, h, k0, nk, w0, c, c_static):
                bank_free(c)
                n = PARTS[h][1] - PARTS[h][0]
                for k in range(nk):
                    w = [WS[s][l][:, (w0 + k) * P:(w0 + k + 1) * P] for l in range(2)]
                    last = three(gb(c_static)[:, 0:n], w, [acts(l, k0 + k, h) for l in range(2)], k == 0, k == nk - 1)
                last.then_inc(s_mm, 1)

            def of_parts(tiles):
                return lambda l, k, h: tiles[h][l][:, k, :]

            def of_attention(l, k, h):
                return AT[l][:, k, PARTS[h][0]:PARTS[h][1]]

            seen = [-1]

            def slab_split(p):
                if seen[0] != p:
                    seen[0] = p
                    pe.wait_ge(s_wlo, p + 1)

            def transposes(c, src):
                if c >= 4:
                    bank_free(c)
                for k in range(4):
                    last = pe.transpose(gb(c)[:, k * P:(k + 1) * P], src(k), ident[:, :])
                last.then_inc(s_mm, 1)

            pe.wait_ge(s_const, 3)
            for j, g in enumerate(SEG1):
                c = C_SEG1 + j
                if g[0] == "ln":
                    _, r, h = g
                    if h == 0:
                        pe.wait_ge(s_xn, r + 1)
                    transposes(c, lambda k: X7[:, r, (4 * h + k) * P:(4 * h + k + 1) * P])
                else:
                    _, p, m, h = g
                    if m == 0:
                        pe.wait_ge(s_ev, 8 if h == 0 else c)
                    slab_split(p)
                    product(p % 2, of_parts(XT), h, 0, NK, 0, c, c)

            with pe.Fori(0, (NH - 2 * EDGE) // 2) as i:
                for s in range(2):
                    pe.wait_ge(s_wlo, P_Q2 + 2 * i + s + 1)
                    for h in range(2):
                        product(s, of_parts(XT), h, 0, NK, 0, C_Q2 + 4 * i + 2 * s + h, C_Q2 + 2 * s + h)
            for j, (_, p, m, h) in enumerate(SEG_Q3):
                slab_split(p)
                product(p % 2, of_parts(XT), h, 0, NK, 0, C_Q3 + j, C_Q3 + j)

            pe.wait_ge(s_plo, 8)

            def wkv(which, k, l, first, n):
                return WKV[which * 4 + k // 2][l][:, (k % 2) * 512 + first:(k % 2) * 512 + first + n]

            with pe.Fori(0, B // 2) as i:
                for j in range(2):
                    b = 2 * i + j
                    pe.wait_ge(s_pad, 2 * j + 2)
                    pe.wait_ge(s_clo, b + 1)
                    pe.wait_ge(s_lat[j], 32 * (i + 1))
                    for u in range(8):
                        bank_free(C_KV + 8 * b + u)
                        dst = gb(C_KV + u)
                        for k in range(NK):
                            if u < 4:
                                last = three(dst[:, 0:KP], [wkv(0, k, l, u * D, D) for l in range(2)],
                                             [HT[j][l][:, k, :] for l in range(2)], k == 0, k == NK - 1)
                            else:
                                last = three(dst[0:KT, :], [HT[j][l][:, k, (u - 4) * KT:(u - 3) * KT] for l in range(2)],
                                             [wkv(1, k, l, 0, 512) for l in range(2)], k == 0, k == NK - 1)
                        last.then_inc(s_mm, 1)

            def av(s, a, ts):
                for t in ts:
                    last = three(AV[a][:, 0:QH],
                                 [VB[s][0:KT, (l * 4 + t) * D:(l * 4 + t + 1) * D] for l in range(2)],
                                 [PT[l][0:KT, t, a * QH:(a + 1) * QH] for l in range(2)], t == 0, t == 3)
                return last

            def attention(n, s, loads, scores, with_av, ev):
                for i in range(QT):
                    if with_av:
                        pe.wait_ge(s_pn, QT * (n - 1) + i + 1)
                        if i < 3 and ev is not None:
                            pe.wait_ge(s_ev, ev - 3 + LAST_USE[i])
                        if i >= 3:
                            pe.wait_ge(s_ptl, QT * (n - 1) + FREED_BY[i])
                        for t in range(4):
                            last = pe.transpose(TB[RING[i]][0:KT, t * P:(t + 1) * P], PR[i][:, t * KT:(t + 1) * KT],
                                                ident[:, :])
                        last.then_inc(s_t, 1)
                    if scores:
                        if i == 0:
                            pe.wait_ge(s_qk[s], loads)
                        if i >= 3 or with_av:
                            pe.wait_ge(s_exp, QT * n + FREED_BY[i])
                        three(SB[RING[i]][:, 0:KP], [QB[s][:, l * QC + i * P:l * QC + (i + 1) * P] for l in range(2)],
                              [KB[s][:, l * KP:(l + 1) * KP] for l in range(2)], True, True).then_inc(s_s, 1)
                    if with_av:
                        if i == 3:
                            pe.wait_ge(s_v[1 - s], loads_of_v(n, s))
                            pe.wait_ge(s_avl, 1 + 2 * (n - 1))
                            if ev is not None:
                                pe.wait_ge(s_ev, ev - 3 + LAST_USE[3])
                        if i == 5:
                            pe.wait_ge(s_ptl, QT * (n - 1) + 4)
                            av(1 - s, 0, [0, 1])
                        if i == 6:
                            av(1 - s, 0, [2, 3]).then_inc(s_av, 1)
                        if i == 6:
                            pe.wait_ge(s_avl, 2 * n)
                            pe.wait_ge(s_ptl, QT * n)
                            av(1 - s, 1, range(4)).then_inc(s_av, 1)

            def loads_of_v(n, s):
                return 8 * (n + 1) if s == 1 else 8 * n

            def loads_of_qk(n, s):
                return 24 * (n + 1) if s == 1 else 24 * (n + 2)

            attention(0, 0, 48, True, False, None)
            with pe.Fori(0, NKV - 1) as kv:
                with pe.Fori(0, B // 2) as i:
                    for j in range(2):
                        n = kv * B + 2 * i + j + 1
                        attention(n, 1 - j, loads_of_qk(n, 1 - j), True, True,
                                  C_WO + kv * 2 * NK if j == 0 else None)
                with pe.Fori(0, NK // 2) as i:
                    for s in range(2):
                        m = 2 * i + s
                        pe.wait_ge(s_wlo, P_WO + kv * NK + m + 1)
                        for h in range(2):
                            pe.wait_ge(s_avl, 2 + 2 * B * kv + (10, 2 * B)[h])
                            product(s, of_attention, h, 0, G, 0, C_WO + kv * 2 * NK + 2 * m + h, C_WO + 2 * s + h)
            with pe.Fori(0, B // 2 - 1) as i:
                for j in range(2):
                    n = (NKV - 1) * B + 2 * i + j + 1
                    attention(n, 1 - j, loads_of_qk(n, 1 - j), True, True, C_SEG2 if j == 0 else None)
            n = NKV * B - 1
            attention(n, 1, loads_of_qk(n, 1), True, True, None)
            attention(n + 1, 0, 0, False, True, None)

            ev_of = {}
            for j, g in enumerate(SEG2):
                c, what = C_SEG2 + j, g[0]
                if what in ("wo", "fc1", "exp", "fc2"):
                    slab_split(g[1])
                if what == "wo":
                    pe.wait_ge(s_avl, 2 + 2 * B * (NKV - 1) + (10 if j == 0 else 2 * B))
                    product(g[1] % 2, of_attention, g[3], 0, G, 0, c, c)
                elif what == "y":
                    if g[2] == 0:
                        pe.wait_ge(s_ev, ev_of["wo", int(g[1] >= 4)])
                    transposes(c, lambda k: Y[:, 4 * g[2] + k, g[1] * P:(g[1] + 1) * P])
                elif what == "n":
                    if g[2] == 0:
                        pe.wait_ge(s_xn, RT + g[1] + 1)
                    transposes(c, lambda k: XN[:, (4 * g[2] + k) * P:(4 * g[2] + k + 1) * P])
                elif what == "fc1":
                    pe.wait_ge(s_ev, ev_of["n", g[3]])
                    product(g[1] % 2, of_parts(X2), g[3], 0, NK, 0, c, c)
                elif what == "logit":
                    pe.wait_ge(s_gs, 1)
                    pe.wait_ge(s_ev, ev_of["n", g[3]])
                    bank_free(c)
                    for k in range(NK):
                        last = three(gb(c)[:, 0:PARTS[g[3]][1] - PARTS[g[3]][0]], [GT[l][:, k, :] for l in range(2)],
                                     [X2[g[3]][l][:, k, :] for l in range(2)], k == 0, k == NK - 1)
                    last.then_inc(s_mm, 1)
                elif what == "logitT":
                    bank_free(c)
                    pe.wait_ge(s_ev, ev_of["logit", 1])
                    for r in range(RT):
                        last = pe.transpose(gb(c)[:, r * NE:(r + 1) * NE], LGT[0:NE, r * P:(r + 1) * P],
                                            ident[0:NE, 0:NE])
                    last.then_inc(s_mm, 1)
                elif what == "routing":
                    bank_free(c)
                    tiles = (range(0, 4), range(4, RT))[g[1]]
                    pe.wait_ge(s_rw, tiles[-1] + 1)
                    for r in tiles:
                        last = pe.transpose(gb(c)[:, (r % 4) * P:(r % 4 + 1) * P], RWREP[:, r, :], ident[:, :])
                    last.then_inc(s_mm, 1)
                elif what == "exp":
                    pe.wait_ge(s_ev, ev_of["fc1", g[3]])
                    product(g[1] % 2, of_parts(IN), g[3], 0, 4, 4 * (g[2] % 2), c, c)
                elif what == "fc2":
                    pe.wait_ge(s_lo, L_FFN - 1 + g[3])
                    product(g[1] % 2, of_parts(IN), g[3], 4, 4, 4 * (g[2] % 2), c, c)
                if len(g) == 4:
                    ev_of[what, g[3]] = c + 1
                if what == "n":
                    ev_of[what, g[1] // 4] = c + 1

            def layer(p0, c0, tiles, ready):
                with pe.Fori(0, NK // 2) as i:
                    for s in range(2):
                        m = 2 * i + s
                        pe.wait_ge(s_wlo, p0 + m + 1)
                        for h in range(2):
                            if ready is not None:
                                pe.wait_ge(s_lo, ready - 1 + h)
                            product(s, of_parts(tiles), h, 0, NK, 0, c0 + 2 * m + h, C_FFN + 2 * s + h)

            layer(P_FFN, C_FFN, X2, None)
            layer(P_FFN + NK, C_FFN + 2 * NK, IN, L_FFN + 2 * NK)
            layer(P_FFN + 2 * NK, C_FFN + 4 * NK, X2, None)

            for j, g in enumerate(SEG3):
                c = C_SEG3 + j
                if g[0] == "down":
                    slab_split(g[1])
                    pe.wait_ge(s_lo, L_FFN + 4 * NK - 1 + g[3])
                    product(g[1] % 2, of_parts(IN), g[3], 0, NK, 0, c, c)
                    ev_of["down", g[3]] = c + 1
                else:
                    if g[2] == 0:
                        pe.wait_ge(s_ev, ev_of["down", int(g[1] >= 4)])
                    transposes(c, lambda k: Y[:, 4 * g[2] + k, g[1] * P:(g[1] + 1) * P])


def kernel(x, ctx_4096, L0_xattn_Wq, L0_xattn_Wk, L0_xattn_Wv, L0_xattn_Wo, L0_ffn_gate_w, L0_ffn_up_w,
           L0_ffn_down_w, L0_ffn_fc1_w, L0_ffn_fc2_w, L0_ffn_expert_w, L0_ffn_ln_gamma, L0_ffn_ln_beta):
    import numpy as np
    import concourse.bacc as bacc
    from concourse import mybir as mb
    from concourse.bass_utils import run_bass_kernel_spmd

    def tiles(w, nk, per):
        w = np.asarray(w)
        k, m = w.shape
        a = w.reshape(k // (nk * P), nk, P, m // (per * P), per, P)
        return a.transpose(0, 3, 2, 4, 1, 5).reshape(-1, P, per * nk * P)

    up, down = np.asarray(L0_ffn_up_w), np.asarray(L0_ffn_down_w)
    slabs = np.concatenate([
        tiles(L0_xattn_Wq, NK, 1), tiles(L0_xattn_Wo, G, 1), tiles(L0_ffn_fc1_w, NK, 1),
        tiles(L0_ffn_expert_w, 4, 2), tiles(L0_ffn_fc2_w, 4, 2),
        tiles(up[:, 0:1024], NK, 1), tiles(down[0:1024], NK, 1),
        tiles(up[:, 1024:2048], NK, 1), tiles(down[1024:2048], NK, 1)])
    wkv = np.concatenate([np.asarray(w).reshape(4, 2, P, 512).transpose(0, 2, 1, 3).reshape(4, P, 1024)
                          for w in (L0_xattn_Wk, L0_xattn_Wv)])
    ctxT = np.asarray(ctx_4096).reshape(B, SC, NK, P).transpose(0, 3, 2, 1)
    gate = np.asarray(L0_ffn_gate_w).reshape(NK, P, NE).transpose(1, 0, 2).reshape(P, NK * NE)
    laid = {"x": np.asarray(x).reshape(ROWS, HID), "ctxT": ctxT, "slabs": slabs, "wkv": wkv, "gate": gate,
            "gamma": L0_ffn_ln_gamma, "beta": L0_ffn_ln_beta}

    nc = bacc.Bacc("TRN2", target_bir_lowering=False, num_devices=1)
    arrays, args = {}, []
    for name, a in laid.items():
        a = np.ascontiguousarray(a)
        arrays[f"in_{name}"] = a
        args.append(nc.dram_tensor(f"in_{name}", a.shape, mb.dt.from_np(a.dtype), kind="ExternalInput").ap())
    args.append(nc.dram_tensor("out", (ROWS, HID), mb.dt.float32, kind="ExternalOutput").ap())
    xattn_ffn(nc, *args)
    r = run_bass_kernel_spmd(nc, [arrays], core_ids=[0])
    return r.results[0]["out"].reshape(B, SQ, HID)
```
